# Optimizing a Trainium2 kernel written in Bass

```python
import numpy as np
import jax
import jax.numpy as jnp

def _softmax(x, axis=-1):
    return jax.nn.softmax(x, axis=axis)

def _gelu(x):
    return jax.nn.gelu(x, approximate=True)

def _silu(x):
    return jax.nn.silu(x)

def _sigmoid(x):
    return jax.nn.sigmoid(x)

def _layernorm(x, axis=-1, eps=1e-05):
    m = jnp.mean(x, axis=axis, keepdims=True)
    v = jnp.var(x, axis=axis, keepdims=True)
    return (x - m) / jnp.sqrt(v + eps)

def _scatter_add(tgt, idx, src, axis=0):
    return tgt.at[idx].add(src)

def _segment_sum(src, seg, n):
    return jax.ops.segment_sum(src, seg, n)
kernel_name = 'mk_seq_postln_d1_jaxref_r8_14185c'

def setup_inputs(seed: int=0):
    np.random.seed(seed)
    _w = jnp.asarray

    def _L0_attn_setup():
        import jax, jax.numpy as jnp
        import numpy as np
        HIDDEN = 256
        NUM_HEADS = 16
        HEAD_SIZE = HIDDEN // NUM_HEADS
        SEQ = 256
        BATCH = 2

        def alibi_causal_bias(seq_len: int, num_heads: int) -> jnp.ndarray:
            i = jnp.arange(seq_len)[:, None]
            j = jnp.arange(seq_len)[None, :]
            dist = -(i - j).astype(jnp.float32)
            causal = jnp.where(j > i, -jnp.inf, 0.0)
            base = jnp.where(j > i, 0.0, dist) + causal
            if num_heads <= 8:
                slopes = jnp.asarray([1.0 / 2 ** k for k in range(num_heads)], jnp.float32)
            else:
                slopes = jnp.asarray([1.0 / 2 ** (k / 2) for k in range(num_heads)], jnp.float32)
            return slopes[None, :, None, None] * dist[None, None] * (j <= i)[None, None] + causal[None, None]
        key = jax.random.key(seed)
        ks = jax.random.split(key, 3)
        sd = 1.0 / np.sqrt(HIDDEN)
        return {'x': jax.random.normal(ks[0], (BATCH, SEQ, HIDDEN), jnp.float32), 'Wqkv': jax.random.normal(ks[1], (HIDDEN, 3 * HIDDEN), jnp.float32) * sd, 'bqkv': jnp.zeros((3 * HIDDEN,), jnp.float32), 'Wo': jax.random.normal(ks[2], (HIDDEN, HIDDEN), jnp.float32) * sd, 'bo': jnp.zeros((HIDDEN,), jnp.float32)}
    _L0_attn_in = _L0_attn_setup()

    def _L0_ffn_setup():
        import jax, jax.numpy as jnp
        import numpy as np
        D_MODEL = 256
        D_EXPERT = 1024
        EPS = 1e-08

        def ternary_quant(w):
            scale = jnp.mean(jnp.abs(w)) + EPS
            q = jnp.clip(jnp.round(w / scale), -1.0, 1.0) * scale
            return w + jax.lax.stop_gradient(q - w)
        key = jax.random.key(seed)
        k_x, k_up, k_gate, k_down = jax.random.split(key, 4)
        std_in = 1.0 / np.sqrt(D_MODEL)
        std_exp = 1.0 / np.sqrt(D_EXPERT)
        return {'x': jax.random.normal(k_x, (4, 256, D_MODEL), dtype=jnp.float32), 'W_up': jax.random.normal(k_up, (D_EXPERT, D_MODEL), dtype=jnp.float32) * std_in, 'W_gate': jax.random.normal(k_gate, (D_EXPERT, D_MODEL), dtype=jnp.float32) * std_in, 'W_down': jax.random.normal(k_down, (D_MODEL, D_EXPERT), dtype=jnp.float32) * std_exp}
    _L0_ffn_in = _L0_ffn_setup()
    _d = {'L0_attn_x': _L0_attn_in['x'], 'L0_attn_Wqkv': _L0_attn_in['Wqkv'], 'L0_attn_bqkv': _L0_attn_in['bqkv'], 'L0_attn_Wo': _L0_attn_in['Wo'], 'L0_attn_bo': _L0_attn_in['bo'], 'L0_ffn_W_up': _L0_ffn_in['W_up'], 'L0_ffn_W_gate': _L0_ffn_in['W_gate'], 'L0_ffn_W_down': _L0_ffn_in['W_down']}
    _x0 = _d['L0_attn_x']
    _d['L0_attn_x'] = jax.random.normal(jax.random.fold_in(jax.random.key(seed), 1), (8, 512, 256), dtype=_x0.dtype)
    del _x0
    return _d

def reference(L0_attn_x, L0_attn_Wqkv, L0_attn_bqkv, L0_attn_Wo, L0_attn_bo, L0_ffn_W_up, L0_ffn_W_gate, L0_ffn_W_down):

    def _L0_attn_ref(x, Wqkv, bqkv, Wo, bo):
        import jax, jax.numpy as jnp
        import numpy as np
        HIDDEN = 256
        NUM_HEADS = 16
        HEAD_SIZE = HIDDEN // NUM_HEADS
        SEQ = 256
        BATCH = 2

        def alibi_causal_bias(seq_len: int, num_heads: int) -> jnp.ndarray:
            i = jnp.arange(seq_len)[:, None]
            j = jnp.arange(seq_len)[None, :]
            dist = -(i - j).astype(jnp.float32)
            causal = jnp.where(j > i, -jnp.inf, 0.0)
            base = jnp.where(j > i, 0.0, dist) + causal
            if num_heads <= 8:
                slopes = jnp.asarray([1.0 / 2 ** k for k in range(num_heads)], jnp.float32)
            else:
                slopes = jnp.asarray([1.0 / 2 ** (k / 2) for k in range(num_heads)], jnp.float32)
            return slopes[None, :, None, None] * dist[None, None] * (j <= i)[None, None] + causal[None, None]
        b, s, h = x.shape
        scale = 1.0 / np.sqrt(HEAD_SIZE)
        qkv = x @ Wqkv + bqkv
        q, k, v = jnp.split(qkv, 3, axis=-1)

        def heads(t):
            return t.reshape(b, s, NUM_HEADS, HEAD_SIZE).transpose(0, 2, 1, 3)
        q, k, v = (heads(q), heads(k), heads(v))
        scores = jnp.einsum('bhid,bhjd->bhij', q, k) * scale
        scores = scores + alibi_causal_bias(s, NUM_HEADS)
        attn = jax.nn.softmax(scores, axis=-1)
        out = jnp.einsum('bhij,bhjd->bhid', attn, v)
        out = out.transpose(0, 2, 1, 3).reshape(b, s, NUM_HEADS * HEAD_SIZE)
        return out @ Wo + bo

    def _L0_ffn_ref(x, W_up, W_gate, W_down):
        import jax, jax.numpy as jnp
        import numpy as np
        D_MODEL = 256
        D_EXPERT = 1024
        EPS = 1e-08

        def ternary_quant(w):
            scale = jnp.mean(jnp.abs(w)) + EPS
            q = jnp.clip(jnp.round(w / scale), -1.0, 1.0) * scale
            return w + jax.lax.stop_gradient(q - w)
        wu = ternary_quant(W_up)
        wg = ternary_quant(W_gate)
        wd = ternary_quant(W_down)
        up = jnp.einsum('bsd,ed->bse', x, wu)
        gate = jnp.einsum('bsd,ed->bse', x, wg)
        hidden = jax.nn.silu(up) * gate
        return jnp.einsum('bse,de->bsd', hidden, wd)
    x = L0_attn_x
    x = _layernorm(x + _L0_attn_ref(x, L0_attn_Wqkv, L0_attn_bqkv, L0_attn_Wo, L0_attn_bo), axis=-1)
    x = _layernorm(x + _L0_ffn_ref(x, L0_ffn_W_up, L0_ffn_W_gate, L0_ffn_W_down), axis=-1)
    return x

_drawn_inputs = setup_inputs


def setup_inputs(seed=0):
    import zlib

    import numpy as np

    out = dict(_drawn_inputs(seed))
    spreads = {'L0_attn_bqkv': (0.0, 0.1), 'L0_attn_bo': (0.0, 0.1)}
    factors = {}
    for name, (base, spread) in spreads.items():
        noise = np.random.default_rng([zlib.crc32(name.encode()), seed]).standard_normal(out[name].shape)
        drawn = base * np.exp(spread * noise) if base else spread * noise
        out[name] = jnp.asarray(drawn.astype(out[name].dtype))
    for name, factor in factors.items():
        out[name] = (out[name] * factor).astype(out[name].dtype)
    return out
```

```python
from contextlib import ExitStack

import numpy as np

import concourse.bass as bass
from concourse import mybir

F32 = mybir.dt.float32
F16 = mybir.dt.float16
BF16 = mybir.dt.bfloat16
U16 = mybir.dt.uint16
ALU = mybir.AluOpType
ACT = mybir.ActivationFunctionType
AX_X = mybir.AxisListType.X

P = 128
BATCH, SEQ, HID = 8, 512, 256
HEADS = 16
DH = HID // HEADS
EXPERT = 1024
TT = SEQ // P
FT = HID // P
ET = EXPERT // P
QUADS = HEADS // 4
QK_TILES = 2 * FT
LN_EPS = 1e-5
QUANT_EPS = 1e-8
MASKED = -1e30
HIDDEN_SCALE = 0.25

PARTS_Q = [0, 0, 0, 1, 1, 2]
PARTS_K = [0, 1, 2, 0, 1, 0]
DATA_ROWS = DH * len(PARTS_Q)
MAX_ROW = 112
CONST_ROWS = P - DATA_ROWS
GROUP = 40

RING = 4
EXP_UNITS = 10
MAX_UNITS = 11


def max_unit(n):
    if n == 0:
        return [0, 1, 2, 3], 0
    if n < 3:
        return [2 * (n - 1), 2 * (n - 1) + 1], 1
    return ([n - 3], 2) if n < 7 else ([n - 7], 3)


def exp_unit(n):
    pair, k = divmod(n, 5)
    if k == 4:
        return [(2 * pair, 2, 0), (2 * pair + 1, 2, 256)]
    head = 2 * pair + k // 2
    return [(head, 0, 0)] if k % 2 == 0 else [(head, 3, 0), (head, 1, 128)]


def piece(head, key_tile):
    for n in range(EXP_UNITS):
        for h, j, col in exp_unit(n):
            if (h, j) == (head, key_tile):
                return n, col


def spread(main, *others):
    keyed = [((i + 0.5) / len(main), 0, i, s) for i, s in enumerate(main)]
    for o, (steps, lo, hi) in enumerate(others):
        keyed += [(lo + (hi - lo) * (i + 0.5) / len(steps), o + 1, i, s) for i, s in enumerate(steps)]
    return [s for *_, s in sorted(keyed, key=lambda x: x[:3])]


def order_of_steps(now, before):
    def if_now(*s):
        return list(s) if now else []

    def if_before(*s):
        return list(s) if before else []

    steps = if_now(("load_x",)) + if_before(("load_res",))
    steps += if_now(("tx", 0), ("tx", 1))
    steps += if_before(*[("pv", 3, j) for j in range(TT)])
    steps += if_now(("qk", 0), ("qk", 1), ("part2", 0), ("stack_write", 0))
    steps += if_before(("nt", 3))
    steps += if_now(("qk", 2), ("part2", 1), ("stack_write", 1), ("stack_read", 0), ("qk", 3))
    steps += if_before(("at", 0), ("at", 1))
    steps += if_now(("part2", 2), ("stack_write", 2), ("v", 0))
    steps += if_before(*[("wo", t) for t in range(TT)])
    steps += if_now(("part2", 3), ("stack_write", 3), ("stack_read", 1))
    steps += if_before(("ln1",))
    steps += if_now(("v", 1))
    steps += if_before(("x1t", 0), ("x1t", 1))
    maxima = [[("max", g, n) for n in range(MAX_UNITS)] + [("mt", g)] for g in range(QUADS)]
    ffn = []
    for m in range(ET + 2):
        if m < ET:
            ffn += [("up", m)]
        if 1 <= m <= ET:
            ffn += [("hidden_hi", m - 1)]
        if m < ET:
            ffn += [("gate", m)]
        if m >= 2:
            ffn += [("down", m - 2)]
    ffn += [("fin", t) for t in range(TT)] + [("ln2",)]
    if before and now:
        steps += spread(ffn, (maxima[0] + maxima[1], 0.35, 1.0))
        steps.append(("store",))
    elif before:
        steps += ffn + [("store",)]
    elif now:
        steps += maxima[0] + [("abs_sums",)] + maxima[1]
    if not now:
        return steps
    for g in range(QUADS):
        exps = [("exp", g, n) for n in range(EXP_UNITS)]
        others = []
        if g:
            others += [([("pv", g - 1, j) for j in range(TT)], 0.25, 0.75), ([("nt", g - 1)], 0.9, 1.0)]
        if g + 2 < QUADS:
            others.append((maxima[g + 2], 0.0, 1.0))
        if g == 2 and not before:
            others.append(([("wsum",), ("ternary", 0), ("ternary", 1), ("ternary", 2)], 0.3, 1.0))
        steps += spread(exps, *others)
    return steps


RING_STEPS = ("tx", "qk", "v", "at", "wo", "x1t", "up", "gate", "mt", "nt", "exp", "wsum")
FIRST, LOOP, LAST = (order_of_steps(True, False), order_of_steps(True, True), order_of_steps(False, True))
RING_FIRST, RING_LOOP = (sum(s[0] in RING_STEPS for s in steps) for steps in (FIRST, LOOP))
assert RING_LOOP % RING == 0


def block_kernel(nc, x, w_qkv, b_qkv, b_qkv_cols, w_o, b_o, w_up_t, w_gate_t, w_down_t, k_const, q_const, out, scratch):
    ctx = ExitStack()
    with ctx:
        def sb(name, shape, dt):
            return ctx.enter_context(nc.sbuf_tensor(name, shape, dt))

        def sem(name):
            return ctx.enter_context(nc.semaphore(name))

        wqkv = sb("wqkv", [P, FT, 3 * HID], F32)
        wo = sb("wo_w", [P, FT, HID], F32)
        tern_up = sb("tern_up", [P, FT, EXPERT], F16)
        tern_gate = sb("tern_gate", [P, FT, EXPERT], F16)
        tern_down = sb("tern_down", [P, ET, HID], F16)
        bias_cols = sb("bias_cols", [P, 3 * FT], F32)
        bias_v = sb("bias_v", [P, 2, HID], F32)
        bias_o = sb("bias_o", [P, HID], F32)
        ident = sb("ident", [P, P], F32)
        ident_bf = sb("ident_bf", [P, P], BF16)
        causal = sb("causal", [P, P], BF16)
        ones = sb("ones", [P, P], F32)
        half_neg = sb("half_neg", [P, TT], F32)
        abs_sums = sb("abs_sums", [P, 3], F32)
        scales = sb("scales", [P, 3], F32)
        thresholds = sb("thresholds", [P, 3], F32)
        neg_thresholds = sb("neg_thresholds", [P, 3], F32)
        tanh_scale = sb("tanh_scale", [P, 1], F32)
        ffn_scale = sb("ffn_scale", [P, 1], F32)
        xin = sb("xin", [P, TT, HID], F32)
        x_t = sb("x_t", [P, FT, SEQ], F32)
        qk_rest = sb("qk_rest", [P, QK_TILES, SEQ], F32)
        qk_parts = sb("qk_parts", [P, QK_TILES, 3, SEQ], BF16)
        q_stack = sb("q_stack", [P, HEADS, SEQ], BF16)
        k_stack = sb("k_stack", [P, HEADS, SEQ], BF16)
        neg_max = sb("neg_max", [P, QUADS, P], F32)
        max_parts = sb("max_parts", [P, QUADS, 2, P], BF16)
        probs = sb("probs", [P, 2, EXP_UNITS, SEQ], F32)
        v_ones = sb("v_ones", [P, TT, HEADS, 32], F32)
        pv_t = sb("pv_t", [P, 2, SEQ], F32)
        inv_sum = sb("inv_sum", [P, 2, TT * 4, 1], F32)
        attn = sb("attn", [P, TT, HID], F32)
        attn_t = sb("attn_t", [P, FT, SEQ], F32)
        res = sb("res", [P, TT, HID], F32)
        z = sb("z", [P, TT, HID], F32)
        stats = sb("stats", [P, TT, 6], F32)
        mean_var = sb("mean_var", [P, TT, 2], F32)
        var_eps = sb("var_eps", [P, TT], F32)
        rstd = sb("rstd", [P, TT], F32)
        x1 = sb("x1", [P, TT, HID], F32)
        x1_hi = sb("x1_hi", [P, FT, SEQ], F16)
        x1_lo = sb("x1_lo", [P, FT, SEQ], F16)
        gating = sb("gating", [P, 4, SEQ], F32)
        hidden = sb("hidden", [P, 2, SEQ], F32)
        hidden_hi = sb("hidden_hi", [P, ET, SEQ], F16)
        hidden_lo = sb("hidden_lo", [P, ET, SEQ], F16)
        y = sb("y", [P, TT, HID], F32)
        stage_up = gating[:, :, :].rearrange("p a b -> p (a b)")
        stage_gate = hidden_hi[:, :, :].rearrange("p a b -> p (a b)").bitcast(F32)
        stage_down = hidden_lo[:, :, :].rearrange("p a b -> p (a b)").bitcast(F32)

        ring = [ctx.enter_context(nc.psum_tensor(f"ring{i}", [P, 512], F32)) for i in range(RING)]
        max_bank = [ctx.enter_context(nc.psum_tensor(f"max_bank{i}", [P, 512], F32)) for i in range(2)]
        acc = [ctx.enter_context(nc.psum_tensor(f"acc{i}", [P, 512], F32)) for i in range(2)]

        ring_filled = [sem(f"ring_filled{i}") for i in range(RING)]
        ring_drained = [sem(f"ring_drained{i}") for i in range(RING)]
        max_filled = [sem(f"max_filled{i}") for i in range(2)]
        max_drained = [sem(f"max_drained{i}") for i in range(2)]
        acc_filled = [sem(f"acc_filled{i}") for i in range(2)]
        acc_drained = [sem(f"acc_drained{i}") for i in range(2)]
        weights_in = [sem(f"weights_in{i}") for i in range(4)]
        dve_passed, pool_passed, sp_passed = sem("dve_passed"), sem("pool_passed"), sem("sp_passed")
        consts_set = sem("consts_set")
        dve_consts = sem("dve_consts")
        pool_step = sem("pool_step")
        q_bias_scaled = sem("q_bias_scaled")
        abs_summed = sem("abs_summed")
        quant_step = sem("quant_step")
        ternary_done = sem("ternary_done")
        x_in = sem("x_in")
        res_in = sem("res_in")
        res_biased = sem("res_biased")
        qk_rest_done = sem("qk_rest_done")
        qk_mid_done = sem("qk_mid_done")
        qk_split = sem("qk_split")
        parts_written = [sem(f"parts_written{t}") for t in range(QK_TILES)]
        stack_in = [sem(f"stack_in{i}") for i in range(FT)]
        max_hi_done = sem("max_hi_done")
        max_in = [sem(f"max_in{g}") for g in range(QUADS)]
        masked = sem("masked")
        inverted = sem("inverted")
        z_done = sem("z_done")
        stats_done = sem("stats_done")
        moments_done = sem("moments_done")
        var_done = sem("var_done")
        rstd_done = sem("rstd_done")
        x1_done = sem("x1_done")
        x1_hi_done = sem("x1_hi_done")
        tanh_done = sem("tanh_done")
        hidden_hi_done = sem("hidden_hi_done")
        hidden_split = sem("hidden_split")
        y_done = sem("y_done")
        y_stored = sem("y_stored")

        STACK_DMAS = 16 * (len(PARTS_Q) + len(PARTS_K))
        MAX_DMAS = 16 * 2

        def at_least(eng, semaphore, per_batch, batch, k):
            if isinstance(batch, int) and per_batch * batch + k == 0:
                return
            eng.wait_ge(semaphore, batch * per_batch + k)

        class Ring:

            def __init__(self, steps, it):
                self.it = it
                self.at = {s: n for n, s in enumerate(s for s in steps if s[0] in RING_STEPS)}

            def slot(self, step):
                if isinstance(self.it, int) and self.it == 0:
                    return self.at[step] % RING
                return (RING_FIRST + self.at[step]) % RING

            def bank(self, step):
                return ring[self.slot(step)]

            def fills(self, step):
                if isinstance(self.it, int) and self.it == 0:
                    return self.at[step] // RING
                return self.it * (RING_LOOP // RING) + (
                    (RING_FIRST + self.at[step]) // RING - RING_LOOP // RING)

            def wait_free(self, eng, step):
                n = self.fills(step)
                if not (isinstance(n, int) and n == 0):
                    eng.wait_ge(ring_drained[self.slot(step)], n)

            def wait_filled(self, eng, step):
                eng.wait_ge(ring_filled[self.slot(step)], self.fills(step) + 1)

            def wait_drained(self, eng, step):
                eng.wait_ge(ring_drained[self.slot(step)], self.fills(step) + 1)

            def filled(self, instruction, step):
                instruction.then_inc(ring_filled[self.slot(step)], 1)

            def drained(self, instruction, step):
                instruction.then_inc(ring_drained[self.slot(step)], 1)

        def max_at(g, n):
            u = g * MAX_UNITS + n
            return u % 2, u // 2

        MAX_PER_BANK = QUADS * MAX_UNITS // 2

        def iterations(eng, body):
            body(FIRST, 0)
            with eng.Fori(1, BATCH) as it:
                body(LOOP, it)
            body(LAST, BATCH)

        block = ctx.enter_context(nc.Block())

        @block.sync
        def _(sp):
            sp.sem_inc(var_done, 2)
            sp.sem_inc(y_stored, 16)
            sp.dma_start(wqkv[:, :, :], w_qkv.rearrange("(t p) n -> p t n", p=P)).then_inc(weights_in[0], 16)
            sp.dma_start(bias_cols[:, :], b_qkv_cols).then_inc(weights_in[0], 16)
            for i in range(2):
                sp.dma_start(bias_v[:, i, :], b_qkv[2 * HID:3 * HID].unsqueeze(0).broadcast_to([P, HID])).then_inc(weights_in[0], 16)
            sp.dma_start(bias_o[:, :], b_o.unsqueeze(0).broadcast_to([P, HID])).then_inc(weights_in[1], 16)
            sp.dma_start(wo[:, :, :], w_o.rearrange("(t p) n -> p t n", p=P)).then_inc(weights_in[1], 16)
            sp.dma_start(k_stack[DATA_ROWS:P, :, :].bitcast(U16), k_const).then_inc(weights_in[2], 16)
            sp.dma_start(q_stack[DATA_ROWS:P, :, :].bitcast(U16),
                         q_const.unsqueeze(1).broadcast_to([CONST_ROWS, HEADS, SEQ])).then_inc(weights_in[2], 16)

            def sp_at_least(semaphore, per_batch, batch, k):
                at_least(sp, semaphore, per_batch, batch, k)
                sp.sem_inc(sp_passed, 1)

            def body(steps, it):
                rg = Ring(steps, it)
                prev = it - 1
                for step in steps:
                    kind = step[0]
                    if kind == "load_x":
                        sp_at_least(qk_split, QK_TILES, it, 0)
                        sp.dma_start(xin[:, :, :], x[it].rearrange("(t p) d -> p t d", p=P)).then_inc(x_in, 16)
                        if isinstance(it, int) and it == 0:
                            sp.dma_start(stage_up, w_up_t.rearrange("(t p) n -> p t n", p=P)).then_inc(weights_in[3], 16)
                            sp.dma_start(stage_gate, w_gate_t.rearrange("(t p) n -> p t n", p=P)).then_inc(weights_in[3], 16)
                            sp.dma_start(stage_down, w_down_t.rearrange("(t p) n -> p t n", p=P)).then_inc(weights_in[3], 16)
                    elif kind == "load_res":
                        sp_at_least(var_done, 2, it, 0)
                        sp.dma_start(res[:, :, :], x[prev].rearrange("(t p) d -> p t d", p=P)).then_inc(res_in, 16)
                    elif kind == "stack_write":
                        t = step[1]
                        sp_at_least(qk_split, QK_TILES, it, t + 1)
                        sp_at_least(stack_in[t // 2], STACK_DMAS, it, 0)
                        sp.dma_start(scratch[t].rearrange("s p n -> p s n"), qk_parts[:, t, :, :]).then_inc(parts_written[t], 16)
                    elif kind == "stack_read":
                        half = step[1]
                        for t, stack, parts in ((2 * half, q_stack, PARTS_Q), (2 * half + 1, k_stack, PARTS_K)):
                            sp_at_least(parts_written[t], 16, it, 16)
                            sp_at_least(masked, 2 * QUADS, it, 0)
                            for r, part in enumerate(parts):
                                sp.dma_start(
                                    stack[DH * r:DH * (r + 1), HEADS // 2 * half:HEADS // 2 * (half + 1), :],
                                    scratch[t, part].rearrange("(h d) n -> d h n", d=DH),
                                ).then_inc(stack_in[half], 16)
                    elif kind == "mt":
                        g = step[1]
                        rg.wait_drained(sp, step)
                        sp.sem_inc(sp_passed, 1)
                        for part in range(2):
                            sp.dma_start(
                                q_stack[MAX_ROW + part:MAX_ROW + part + 1, 4 * g:4 * g + 4, :],
                                max_parts[0:4 * TT, g, part, :],
                            ).then_inc(max_in[g], 16)
                    elif kind == "store":
                        sp_at_least(y_done, TT, prev, TT)
                        sp.dma_start(out[prev].rearrange("(t p) d -> p t d", p=P), y[:, :, :]).then_inc(y_stored, 16)

            iterations(sp, body)
            sp.wait_ge(y_stored, 16 * (BATCH + 1))
            for t in range(QK_TILES):
                sp.wait_ge(parts_written[t], 16 * BATCH)

        @block.tensor
        def _(pe):
            def body(steps, it):
                rg = Ring(steps, it)
                prev = it - 1
                first = isinstance(it, int) and it == 0
                for step in steps:
                    kind = step[0]
                    if kind in RING_STEPS:
                        rg.wait_free(pe, step)
                        bank = rg.bank(step)
                    if kind == "tx":
                        f = step[1]
                        if f == 0:
                            at_least(pe, x_in, 16, it, 16)
                            if first:
                                pe.wait_ge(consts_set, 1)
                        for t in range(TT):
                            mm = pe.transpose(bank[:, P * t:P * (t + 1)], xin[:, t, P * f:P * (f + 1)], ident[:, :])
                        rg.filled(mm, step)
                    elif kind == "qk":
                        t = step[1]
                        if t == 0:
                            rg.wait_drained(pe, ("tx", 0))
                            rg.wait_drained(pe, ("tx", 1))
                            if first:
                                pe.wait_ge(weights_in[0], 64)
                        col = HID * (t % 2) + P * (t // 2)
                        for f in range(FT):
                            mm = pe.matmul(bank[:, :], wqkv[:, f, col:col + P], x_t[:, f, :], start=(f == 0), stop=(f == FT - 1))
                        rg.filled(mm, step)
                    elif kind == "v":
                        for i in range(2):
                            t = 2 * step[1] + i
                            for f in range(FT):
                                mm = pe.matmul(bank[:, HID * i:HID * (i + 1)], x_t[:, f, P * t:P * (t + 1)],
                                               wqkv[:, f, 2 * HID:3 * HID], start=(f == 0), stop=(f == FT - 1))
                        rg.filled(mm, step)
                    elif kind == "max":
                        _, g, n = step
                        k, use = max_at(g, n)
                        if n == 0 and g % 2 == 0:
                            at_least(pe, stack_in[g // 2], STACK_DMAS, it, STACK_DMAS)
                            if first:
                                pe.wait_ge(weights_in[2], 32)
                        at_least(pe, max_drained[k], MAX_PER_BANK, it, use)
                        heads, tile = max_unit(n)
                        width = P * (tile + 1)
                        for i, h in enumerate(heads):
                            o = max_bank[k][:, width * i:width * (i + 1)]
                            pe.matmul(o, q_stack[0:MAX_ROW, 4 * g + h, P * tile:P * (tile + 1)],
                                      k_stack[0:MAX_ROW, 4 * g + h, 0:width], start=True, stop=False)
                            mm = pe.matmul(o[:, width - P:width], ident_bf[:, :], causal[:, :], start=False, stop=True)
                        mm.then_inc(max_filled[k], 1)
                    elif kind == "mt":
                        g = step[1]
                        if first and g == 0:
                            pe.wait_ge(dve_consts, 1)
                        for n in (MAX_UNITS - 2, MAX_UNITS - 1):
                            k, use = max_at(g, n)
                            at_least(pe, max_drained[k], MAX_PER_BANK, it, use + 1)
                        rg.filled(pe.transpose(bank[:, 0:P], neg_max[:, g, :], ident[:, :]), step)
                    elif kind == "exp":
                        _, g, n = step
                        if n == 0:
                            at_least(pe, max_in[g], MAX_DMAS, it, MAX_DMAS)
                        for h, j, col in exp_unit(n):
                            mm = pe.matmul(bank[:, col:col + SEQ - P * j], k_stack[:, 4 * g + h, P * j:P * (j + 1)],
                                           q_stack[:, 4 * g + h, P * j:SEQ], start=True, stop=True)
                        rg.filled(mm, step)
                    elif kind == "pv":
                        _, g, j = step
                        batch = prev if g == 3 else it
                        if j == 0:
                            at_least(pe, masked, 2 * QUADS, batch, 2 * (g + 1))
                            at_least(pe, acc_drained[g % 2], 3, batch, g // 2)
                            if g == 0:
                                rg.wait_drained(pe, ("v", 0))
                                rg.wait_drained(pe, ("v", 1))
                        for h in range(4):
                            n, col = piece(h, j)
                            mm = pe.matmul(acc[g % 2][32 * h:32 * (h + 1), P * j:SEQ], v_ones[:, j, 4 * g + h, :],
                                           probs[:, g % 2, n, col:col + SEQ - P * j], start=(j == 0), stop=(j == TT - 1))
                        if j == TT - 1:
                            mm.then_inc(acc_filled[g % 2], 1)
                    elif kind == "nt":
                        g = step[1]
                        batch = prev if g == 3 else it
                        at_least(pe, acc_drained[g % 2], 3, batch, g // 2 + 1)
                        for t in range(TT):
                            mm = pe.transpose(bank[:, P * t:P * (t + 1)], pv_t[:, g % 2, P * t:P * (t + 1)], ident[:, :])
                        rg.filled(mm, step)
                    elif kind == "at":
                        f = step[1]
                        if f == 0:
                            rg.wait_drained(pe, ("nt", 3))
                        for t in range(TT):
                            mm = pe.transpose(bank[:, P * t:P * (t + 1)], attn[:, t, P * f:P * (f + 1)], ident[:, :])
                        rg.filled(mm, step)
                    elif kind == "wo":
                        t = step[1]
                        if t == 0:
                            rg.wait_drained(pe, ("at", 0))
                            rg.wait_drained(pe, ("at", 1))
                            pe.wait_ge(weights_in[1], 32)
                        for f in range(FT):
                            mm = pe.matmul(bank[:, 0:HID], attn_t[:, f, P * t:P * (t + 1)], wo[:, f, :],
                                           start=(f == 0), stop=(f == FT - 1))
                        rg.filled(mm, step)
                    elif kind == "x1t":
                        f = step[1]
                        if f == 0:
                            at_least(pe, x1_done, TT, prev, TT)
                        for t in range(TT):
                            mm = pe.transpose(bank[:, P * t:P * (t + 1)], x1[:, t, P * f:P * (f + 1)], ident[:, :])
                        rg.filled(mm, step)
                    elif kind in ("up", "gate"):
                        m = step[1]
                        if step == ("up", 0):
                            rg.wait_drained(pe, ("x1t", 0))
                            rg.wait_drained(pe, ("x1t", 1))
                            pe.wait_ge(ternary_done, 3)
                        w = tern_up if kind == "up" else tern_gate
                        for f in range(FT):
                            for part in (x1_hi, x1_lo):
                                mm = pe.matmul(bank[:, :], w[:, f, P * m:P * (m + 1)], part[:, f, :],
                                               start=(f == 0 and part is x1_hi), stop=(f == FT - 1 and part is x1_lo))
                        rg.filled(mm, step)
                    elif kind == "down":
                        m = step[1]
                        if m == 0:
                            for k in range(2):
                                at_least(pe, acc_drained[k], 3, prev, 2)
                        at_least(pe, hidden_split, ET, prev, m + 1)
                        for t in range(TT):
                            for part in (hidden_hi, hidden_lo):
                                mm = pe.matmul(acc[t // 2][:, HID * (t % 2):HID * (t % 2 + 1)], part[:, m, P * t:P * (t + 1)],
                                               tern_down[:, m, :], start=(m == 0 and part is hidden_hi and t % 2 == 0),
                                               stop=(m == ET - 1 and part is hidden_lo), skip_group_check=True)
                            if m == ET - 1 and t % 2 == 1:
                                mm.then_inc(acc_filled[t // 2], 1)
                    elif kind == "wsum":
                        pe.wait_ge(abs_summed, 3)
                        pe.wait_ge(dve_consts, 1)
                        rg.filled(pe.matmul(bank[:, 0:3], ones[:, :], abs_sums[:, :], start=True, stop=True), step)

            iterations(pe, body)

        @block.scalar
        def _(act):
            def body(steps, it):
                rg = Ring(steps, it)
                prev = it - 1
                first = isinstance(it, int) and it == 0
                for step in steps:
                    kind = step[0]
                    if kind == "tx":
                        rg.wait_filled(act, step)
                        rg.drained(act.activation(x_t[:, step[1], :], rg.bank(step)[:, :], ACT.Copy), step)
                    elif kind == "qk":
                        t = step[1]
                        if first and t == 0:
                            act.wait_ge(q_bias_scaled, 1)
                        scale = DH ** -0.5 if t % 2 == 0 else 1.0
                        bias = bias_cols[:, FT * (t % 2) + t // 2:FT * (t % 2) + t // 2 + 1]
                        at_least(act, qk_split, QK_TILES, it, 0)
                        at_least(act, parts_written[t], 16, it, 0)
                        rg.wait_filled(act, step)
                        act.activation(qk_rest[:, t, :], rg.bank(step)[:, :], ACT.Identity, bias=bias, scale=scale)
                        rg.drained(act.activation(qk_parts[:, t, 0, :], rg.bank(step)[:, :], ACT.Identity, bias=bias,
                                                  scale=scale), step)
                    elif kind == "exp":
                        _, g, n = step
                        if n == 0:
                            at_least(act, acc_filled[g % 2], 3, it, g // 2)
                        rg.wait_filled(act, step)
                        rg.drained(act.activation(probs[:, g % 2, n, :], rg.bank(step)[:, :], ACT.Exp), step)
                    elif kind == "pv" and step[2] == TT - 1:
                        g = step[1]
                        batch = prev if g == 3 else it
                        at_least(act, acc_filled[g % 2], 3, batch, g // 2 + 1)
                        act.activation(pv_t[:, g % 2, :], acc[g % 2][:, :], ACT.Copy).then_inc(acc_drained[g % 2], 1)
                    elif kind == "at":
                        rg.wait_filled(act, step)
                        rg.drained(act.activation(attn_t[:, step[1], :], rg.bank(step)[:, :], ACT.Copy), step)
                    elif kind == "x1t":
                        rg.wait_filled(act, step)
                        act.activation(x1_hi[:, step[1], :], rg.bank(step)[:, :], ACT.Copy).then_inc(x1_hi_done, 1)
                    elif kind == "up":
                        m = step[1]
                        if m >= 2:
                            rg.wait_drained(act, ("up", m - 2))
                        rg.wait_filled(act, step)
                        act.activation(gating[:, m % 2, :], rg.bank(step)[:, :], ACT.Tanh,
                                       scale=tanh_scale[:, 0:1]).then_inc(tanh_done, 1)
                    elif kind == "hidden_hi":
                        m = step[1]
                        rg.wait_drained(act, ("gate", m))
                        act.activation(hidden_hi[:, m, :], hidden[:, m % 2, :], ACT.Copy).then_inc(hidden_hi_done, 1)

            iterations(act, body)

        @block.vector
        def _(dve):
            dve.memset(ones[:, :], 1.0)
            dve.memset(half_neg[:, :], -0.5)
            dve.memset(neg_max[:, :, :], 0.0)
            dve.memset(v_ones[:, :, :, :], 1.0).then_inc(dve_consts, 1)
            dve.wait_ge(dve_consts, 1)
            dve.wait_ge(weights_in[0], 64)
            dve.tensor_scalar(bias_cols[:, 0:FT], bias_cols[:, 0:FT], DH ** -0.5, None, ALU.mult).then_inc(q_bias_scaled, 1)

            def normalise(batch, which, target, done):
                at_least(dve, rstd_done, 2, batch, which + 1)
                for t in range(TT):
                    dve.tensor_scalar(target[:, t, :], z[:, t, :], mean_var[:, t, 0:1], rstd[:, t:t + 1],
                                      ALU.subtract, ALU.mult).then_inc(done, 1)

            def variances(batch, which):
                at_least(dve, moments_done, 2 * TT, batch, (which + 1) * TT)
                dve.tensor_scalar(var_eps[:, :], mean_var[:, :, 1], LN_EPS, None, ALU.add).then_inc(var_done, 1)

            def body(steps, it):
                rg = Ring(steps, it)
                prev = it - 1
                first = isinstance(it, int) and it == 0
                for step in steps:
                    kind = step[0]
                    if kind == "part2":
                        t = step[1]
                        at_least(dve, qk_rest_done, QK_TILES, it, t + 1)
                        dve.tensor_copy(qk_parts[:, t, 1, :], qk_rest[:, t, :]).then_inc(qk_mid_done, 1)
                    elif kind == "v":
                        u = step[1]
                        if first and u == 0:
                            dve.wait_ge(dve_consts, 1)
                        rg.wait_filled(dve, step)
                        rg.drained(dve.tensor_tensor(
                            v_ones[:, 2 * u:2 * u + 2, :, 0:DH].rearrange("p t h d -> p (t h) d"),
                            rg.bank(step)[:, :].rearrange("p (s d) -> p s d", d=DH),
                            bias_v[:, :, :].rearrange("p t (h d) -> p (t h) d", d=DH), ALU.add), step)
                    elif kind == "max":
                        _, g, n = step
                        k, use = max_at(g, n)
                        heads, tile = max_unit(n)
                        width = P * (tile + 1)
                        at_least(dve, max_filled[k], MAX_PER_BANK, it, use + 1)
                        first_col = 4 * heads[0] + tile
                        dve.tensor_reduce(
                            neg_max[:, g, first_col:first_col + 4 * (len(heads) - 1) + 1:4],
                            max_bank[k][:, 0:width * len(heads)].rearrange("p (h j) -> p h j", j=width),
                            AX_X, ALU.max, negate=True).then_inc(max_drained[k], 1)
                    elif kind == "mt":
                        g = step[1]
                        at_least(dve, max_in[g], MAX_DMAS, it, 0)
                        rg.wait_filled(dve, step)
                        m_t = rg.bank(step)[0:4 * TT, 0:P]
                        dve.tensor_copy(max_parts[0:4 * TT, g, 0, :], m_t).then_inc(max_hi_done, 1)
                        at_least(dve, max_hi_done, QUADS, it, g + 1)
                        rg.drained(dve.tensor_tensor(max_parts[0:4 * TT, g, 1, :], m_t, max_parts[0:4 * TT, g, 0, :],
                                                     ALU.subtract), step)
                    elif kind == "nt":
                        g = step[1]
                        batch = prev if g == 3 else it
                        rg.wait_filled(dve, step)
                        heads = rg.bank(step)[:, :].rearrange("p (s c) -> p s c", c=32)
                        dve.reciprocal(inv_sum[:, g % 2, :, :], heads[:, :, DH:DH + 1]).then_inc(inverted, 1)
                        at_least(dve, inverted, QUADS, batch, g + 1)
                        rg.drained(dve.tensor_tensor(
                            attn[:, :, 4 * DH * g:4 * DH * (g + 1)].rearrange("p t (h d) -> p t h d", d=DH),
                            heads[:, :, 0:DH].rearrange("p (t h) d -> p t h d", t=TT),
                            inv_sum[:, g % 2, :, :].rearrange("p (t h) o -> p t h o", t=TT).broadcast_to([P, TT, 4, DH]),
                            ALU.mult), step)
                    elif kind == "wo":
                        t = step[1]
                        if t == 0:
                            at_least(dve, res_biased, 1, prev, 1)
                        rg.wait_filled(dve, step)
                        rg.drained(dve.tensor_tensor(z[:, t, :], rg.bank(step)[:, 0:HID], res[:, t, :], ALU.add), step)
                        rg.wait_drained(dve, step)
                        dve.bn_stats(stats[:, t, :], z[:, t, :]).then_inc(stats_done, 1)
                        at_least(dve, stats_done, TT + 2, prev, t + 1)
                        dve.sem_inc(dve_passed, 1)
                        dve.bn_aggr(mean_var[:, t, :], stats[:, t, :]).then_inc(moments_done, 1)
                        if t == TT - 1:
                            variances(prev, 0)
                    elif kind == "ln1":
                        normalise(prev, 0, x1, x1_done)
                    elif kind == "x1t":
                        f = step[1]
                        at_least(dve, x1_hi_done, FT, prev, f + 1)
                        rg.drained(dve.tensor_tensor(x1_lo[:, f, :], rg.bank(step)[:, :], x1_hi[:, f, :], ALU.subtract), step)
                    elif kind == "up":
                        m = step[1]
                        at_least(dve, tanh_done, ET, prev, m + 1)
                        rg.drained(dve.scalar_tensor_tensor(
                            out=gating[:, 2 + m % 2, :], in0=gating[:, m % 2, :], scalar=1.0, in1=rg.bank(step)[:, :],
                            op0=ALU.add, op1=ALU.mult), step)
                    elif kind == "gate":
                        m = step[1]
                        if m >= 2:
                            at_least(dve, hidden_split, ET, prev, m - 1)
                        rg.wait_filled(dve, step)
                        rg.wait_drained(dve, ("up", m))
                        rg.drained(dve.scalar_tensor_tensor(
                            out=hidden[:, m % 2, :], in0=gating[:, 2 + m % 2, :], scalar=HIDDEN_SCALE,
                            in1=rg.bank(step)[:, :], op0=ALU.mult, op1=ALU.mult), step)
                    elif kind == "fin":
                        t = step[1]
                        if t % 2 == 0:
                            at_least(dve, acc_filled[t // 2], 3, prev, 3)
                        dve.scalar_tensor_tensor(
                            out=z[:, t, :], in0=acc[t // 2][:, HID * (t % 2):HID * (t % 2 + 1)], scalar=ffn_scale[:, 0:1],
                            in1=x1[:, t, :], op0=ALU.mult, op1=ALU.add).then_inc(z_done, 1)
                        at_least(dve, z_done, TT, prev, t + 1)
                        ins = dve.bn_stats(stats[:, t, :], z[:, t, :])
                        if t % 2 == 0:
                            ins.then_inc(stats_done, 1)
                            at_least(dve, stats_done, TT + 2, prev, TT + t // 2 + 1)
                        else:
                            ins.then_inc(acc_drained[t // 2], 1)
                            at_least(dve, acc_drained[t // 2], 3, prev, 3)
                        dve.sem_inc(dve_passed, 1)
                        dve.bn_aggr(mean_var[:, t, :], stats[:, t, :]).then_inc(moments_done, 1)
                        if t == TT - 1:
                            variances(prev, 1)
                    elif kind == "ln2":
                        at_least(dve, y_stored, 16, it, 0)
                        normalise(prev, 1, y, y_done)

                    elif kind == "abs_sums":
                        dve.wait_ge(weights_in[3], 48)
                        for i, w in enumerate((stage_up, stage_gate, stage_down)):
                            dve.tensor_reduce(abs_sums[:, i:i + 1], w, AX_X, ALU.add,
                                              apply_absolute_value=True).then_inc(abs_summed, 1)
                    elif kind == "wsum":
                        rg.wait_filled(dve, step)
                        rg.drained(dve.tensor_scalar(scales[:, :], rg.bank(step)[:, 0:3], 1.0 / (EXPERT * HID), QUANT_EPS,
                                                     ALU.mult, ALU.add), step)
                        rg.wait_drained(dve, step)
                        dve.tensor_scalar(thresholds[:, :], scales[:, :], 0.5, None, ALU.mult).then_inc(quant_step, 1)
                        dve.tensor_scalar(neg_thresholds[:, :], scales[:, :], -0.5, None, ALU.mult).then_inc(quant_step, 1)
                        dve.tensor_scalar(tanh_scale[:, :], scales[:, 0:1], 0.5, None, ALU.mult).then_inc(quant_step, 1)
                        dve.tensor_scalar(ffn_scale[:, :], scales[:, 1:2], scales[:, 2:3], 1.0 / HIDDEN_SCALE,
                                          ALU.mult, ALU.mult).then_inc(quant_step, 1)
                        dve.wait_ge(quant_step, 4)
                        dve.tensor_tensor(ffn_scale[:, :], ffn_scale[:, :], tanh_scale[:, :], ALU.mult).then_inc(quant_step, 1)
                    elif kind == "ternary":
                        i = step[1]
                        w = (stage_up, stage_gate, stage_down)[i]
                        t = (tern_up, tern_gate, tern_down)[i][:, :, :].rearrange("p a b -> p (a b)")
                        dve.tensor_scalar(t, w, neg_thresholds[:, i:i + 1], None, ALU.is_lt).then_inc(quant_step, 1)
                        dve.wait_ge(quant_step, 6 + i)
                        dve.scalar_tensor_tensor(out=t, in0=w, scalar=thresholds[:, i:i + 1], in1=t,
                                                 op0=ALU.is_gt, op1=ALU.subtract).then_inc(ternary_done, 1)

            iterations(dve, body)

        @block.gpsimd
        def _(pool):
            pool.memset(ident[:, :], 0.0).then_inc(pool_step, 1)
            pool.memset(causal[:, :], 0.0).then_inc(pool_step, 1)
            pool.wait_ge(pool_step, 2)
            pool.affine_select(out=ident[:, :], in_=ident[:, :], compare_op=ALU.not_equal, fill=1.0, base=0,
                               pattern=[[-1, P]], channel_multiplier=1).then_inc(pool_step, 1)
            pool.affine_select(out=causal[:, :], in_=causal[:, :], compare_op=ALU.is_ge, fill=MASKED, base=0,
                               pattern=[[-1, P]], channel_multiplier=1).then_inc(pool_step, 1)
            pool.wait_ge(pool_step, 4)
            pool.tensor_copy(ident_bf[:, :], ident[:, :]).then_inc(consts_set, 1)
            pool.wait_ge(dve_consts, 1)

            def keep_past(v, blocks):
                return pool.affine_select(out=v, in_=v, compare_op=ALU.is_ge, fill=0.0, base=0,
                                          pattern=([[0, blocks]] if blocks > 1 else []) + [[1, P]], channel_multiplier=-1)

            def body(steps, it):
                rg = Ring(steps, it)
                prev = it - 1
                for step in steps:
                    kind = step[0]
                    if kind == "load_res":
                        at_least(pool, res_in, 16, prev, 16)
                        pool.wait_ge(weights_in[1], 32)
                        for t in range(TT):
                            ins = pool.tensor_tensor(res[:, t, :], res[:, t, :], bias_o[:, :], ALU.add)
                        ins.then_inc(res_biased, 1)
                    elif kind == "qk":
                        t = step[1]
                        rg.wait_drained(pool, step)
                        pool.tensor_tensor(qk_rest[:, t, :], qk_rest[:, t, :], qk_parts[:, t, 0, :],
                                           ALU.subtract).then_inc(qk_rest_done, 1)
                    elif kind == "part2":
                        t = step[1]
                        at_least(pool, qk_mid_done, QK_TILES, it, t + 1)
                        pool.tensor_tensor(qk_parts[:, t, 2, :], qk_rest[:, t, :], qk_parts[:, t, 1, :],
                                           ALU.subtract).then_inc(qk_split, 1)
                    elif kind in ("ln1", "ln2"):
                        at_least(pool, var_done, 2, it, 1 if kind == "ln1" else 2)
                        pool.tensor_tensor(rstd[:, :], var_eps[:, :], half_neg[:, :], ALU.pow).then_inc(rstd_done, 1)
                    elif kind == "hidden_hi":
                        m = step[1]
                        at_least(pool, hidden_hi_done, ET, prev, m + 1)
                        pool.tensor_tensor(hidden_lo[:, m, :], hidden[:, m % 2, :], hidden_hi[:, m, :],
                                           ALU.subtract).then_inc(hidden_split, 1)
                    elif kind == "exp" and step[2] % 5 == 4:
                        _, g, n = step
                        rg.wait_drained(pool, step)
                        pool.sem_inc(pool_passed, 1)
                        pair = probs[:, g % 2, n - 4:n + 1, :]
                        keep_past(pair[:, :, 0:P], 5)
                        keep_past(pair[:, 1:4:2, P:2 * P], 2)
                        keep_past(pair[:, 4, 2 * P:3 * P], 1).then_inc(masked, 1)

            iterations(pool, body)


def bf16_parts(values):
    parts = []
    for _ in range(3):
        bits = values.view(np.uint32) & np.uint32(0xFFFF0000)
        parts.append((bits >> np.uint32(16)).astype(np.uint16))
        values = values - bits.view(np.float32)
    return parts


def constant_rows():
    one, masked = 0x3F80, bf16_parts(np.asarray([MASKED], np.float32))[0][0]
    slopes = np.asarray([1.0 / 2 ** (k / 2) for k in range(HEADS)], np.float32)
    position = np.arange(SEQ)
    k_rows = np.zeros((CONST_ROWS, HEADS, SEQ), np.uint16)
    q_rows = np.zeros((CONST_ROWS, SEQ), np.uint16)
    k_rows[0:3] = bf16_parts(slopes[:, None] * position.astype(np.float32)[None, :])
    q_rows[0:3] = one
    for group in range(MAX_ROW - DATA_ROWS - 3):
        q_rows[3 + group, position // GROUP == group] = one
        k_rows[3 + group, :, position // GROUP > group] = masked
    k_rows[MAX_ROW - DATA_ROWS:MAX_ROW - DATA_ROWS + 2] = one
    return k_rows, q_rows


def kernel(L0_attn_x, L0_attn_Wqkv, L0_attn_bqkv, L0_attn_Wo, L0_attn_bo, L0_ffn_W_up, L0_ffn_W_gate, L0_ffn_W_down):
    import concourse.bacc as bacc
    from concourse.bass_utils import run_bass_kernel_spmd

    k_rows, q_rows = constant_rows()
    arrays = {
        "x_dram": np.ascontiguousarray(L0_attn_x),
        "w_qkv_dram": np.ascontiguousarray(L0_attn_Wqkv),
        "b_qkv_dram": np.ascontiguousarray(L0_attn_bqkv),
        "b_qkv_cols_dram": np.ascontiguousarray(np.asarray(L0_attn_bqkv).reshape(3 * FT, P).T),
        "w_o_dram": np.ascontiguousarray(L0_attn_Wo),
        "b_o_dram": np.ascontiguousarray(L0_attn_bo),
        "w_up_dram": np.ascontiguousarray(np.asarray(L0_ffn_W_up).T),
        "w_gate_dram": np.ascontiguousarray(np.asarray(L0_ffn_W_gate).T),
        "w_down_dram": np.ascontiguousarray(np.asarray(L0_ffn_W_down).T),
        "k_const_dram": k_rows,
        "q_const_dram": q_rows,
    }
    nc = bacc.Bacc("TRN2", target_bir_lowering=False, num_devices=1)
    args = [nc.dram_tensor(name, a.shape, mybir.dt.from_np(a.dtype), kind="ExternalInput").ap() for name, a in arrays.items()]
    out = nc.dram_tensor("out_dram", (BATCH, SEQ, HID), F32, kind="ExternalOutput").ap()
    scratch = nc.dram_tensor("qk_scratch", (QK_TILES, 3, P, SEQ), BF16, kind="Internal").ap()
    block_kernel(nc, *args, out, scratch)
    r = run_bass_kernel_spmd(nc, [arrays], core_ids=[0])
    return r.results[0]["out_dram"]
```

```python
from contextlib import ExitStack

import numpy as np

import concourse.bass as bass
from concourse import mybir

F32 = mybir.dt.float32
F16 = mybir.dt.float16
BF16 = mybir.dt.bfloat16
U16 = mybir.dt.uint16
ALU = mybir.AluOpType
ACT = mybir.ActivationFunctionType
AX_X = mybir.AxisListType.X

P = 128
BATCH, SEQ, HID = 8, 512, 256
HEADS = 16
DH = HID // HEADS
EXPERT = 1024
TT = SEQ // P
FT = HID // P
ET = EXPERT // P
QUADS = HEADS // 4
QK_TILES = 2 * FT
LN_EPS = 1e-5
QUANT_EPS = 1e-8
MASKED = -1e30
HIDDEN_SCALE = 0.25

STACK_RUNS = [(0, 3), (0, 2), (0, 1)]
DATA_ROWS = DH * sum(n for _, n in STACK_RUNS)
MAX_ROW = 112
CONST_ROWS = P - DATA_ROWS
GROUP = 40

RING = 4
EXP_UNITS = 10
MAX_UNITS = 11


def max_unit(n):
    if n == 0:
        return [0, 1, 2, 3], 0
    if n < 3:
        return [2 * (n - 1), 2 * (n - 1) + 1], 1
    return ([n - 3], 2) if n < 7 else ([n - 7], 3)


def exp_unit(n):
    pair, k = divmod(n, 5)
    if k == 4:
        return [(2 * pair, 2, 0), (2 * pair + 1, 2, 256)]
    head = 2 * pair + k // 2
    return [(head, 0, 0)] if k % 2 == 0 else [(head, 3, 0), (head, 1, 128)]


def piece(head, key_tile):
    for n in range(EXP_UNITS):
        for h, j, col in exp_unit(n):
            if (h, j) == (head, key_tile):
                return n, col


def weave(*parts):
    keyed = []
    for p, (steps, lo, hi) in enumerate(parts):
        keyed += [(lo + (hi - lo) * (i + 0.5) / len(steps), p, i, s) for i, s in enumerate(steps)]
    return [s for *_, s in sorted(keyed, key=lambda x: x[:3])]


def of_batch_before(step):
    return step[0] == "exp" and step[1] == 3 or step[0] in ("pv", "nt") and step[1] >= 2


def order_of_steps(now, before):
    def if_now(*s):
        return list(s) if now else []

    def if_before(*s):
        return list(s) if before else []

    def exps(g, lo, hi):
        return [("exp", g, n) for n in range(lo, hi)]

    def pvs(g):
        return [("pv", g, j) for j in range(TT)]

    def take_max(units):
        return [s for u in units for s in ([u, ("take", *u[1:])] if u[0] == "max" else [u])]

    steps = if_now(("load_x",)) + if_before(("load_res",))
    steps += if_now(("tx", 0), ("tx", 1))
    steps += if_before(("exp", 3, 0), ("pv", 2, 0), *exps(3, 1, 3), ("pv", 2, 1))
    steps += if_now(("qk", 0))
    steps += if_before(*exps(3, 3, 5), ("pv", 2, 2), ("pv", 2, 3), ("exp", 3, 5))
    steps += if_now(("split", 0), ("stack_write", 0), ("qk", 1))
    steps += if_before(("exp", 3, 6))
    steps += if_now(("split", 1), ("stack_write", 1), ("stack_read", 0))
    steps += if_before(("exp", 3, 7), ("nt", 2), *exps(3, 8, 10))
    steps += if_now(("qk", 2), ("split", 2))
    steps += if_before(("at", 0), *pvs(3))
    steps += if_now(("v", 0), ("v_out", 0), ("v", 1), ("v_out", 1), ("stack_write", 2))
    if now and not before:
        steps += [("abs_sums",), ("wsum",), ("ternary", 0)]
    steps += if_before(("nt", 3), ("wo", 0, 0), ("at", 1), ("wo", 1, 0), ("wo", 0, 1), ("wo", 1, 1))
    if before and now:
        steps += [("max", 0, 0), ("max", 0, 1), ("take", 0, 0), ("v", 2), ("v_out", 2), ("v", 3), ("v_out", 3), ("ln1",),
                  ("qk", 3), ("max", 0, 2), ("x1t", 0), ("x1t", 1), ("take", 0, 1), ("max", 0, 3),
                  ("x1_lo", 0), ("x1_lo", 1), ("take", 0, 2), ("take", 0, 3), ("split", 3)]
    elif now:
        steps += [("v", 2), ("v_out", 2), ("v", 3), ("v_out", 3), ("qk", 3), ("split", 3)]
    else:
        steps += [("ln1",), ("x1t", 0), ("x1t", 1), ("x1_lo", 0), ("x1_lo", 1)]

    maxima = []
    for g in range(QUADS):
        maxima += [("max", g, n) for n in range(4 if before and g == 0 else 0, MAX_UNITS)]
        if g:
            maxima.insert(-MAX_UNITS + 3, ("mt", g - 1))
    early = maxima.index(("mt", 1)) + 1
    ffn = []
    for m in range(ET):
        ffn += [("up", m)] + [("hidden_hi", m - 1)] * (m > 0) + [("gate", m), ("swish", m)]
        ffn += [("down", m - 2)] * (m > 1) + [("swiglu", m)]
    ffn += [("hidden_hi", ET - 1), ("down", ET - 2)]
    woven = []
    if before:
        woven += [
            (ffn, 0.0, 0.6), ([("down", ET - 1)], 0.64, 0.65),
            ([("ffn_sum", u) for u in range(2)], 0.67, 0.70),
            ([("ffn_stats", t) for t in range(TT)] + [("ln2",)], 0.85, 0.99),
        ]
    if now:
        woven += [
            ([("stack_write", 3), ("stack_read", 1)], 0.05, 0.07),
            (take_max(maxima[:early]), 0.0, 0.63), (take_max(maxima[early:]), 0.63, 0.93), ([("mt", 3)], 0.96, 0.97),
            (exps(0, 0, EXP_UNITS), 0.42, 0.64), (exps(1, 0, EXP_UNITS), 0.70, 0.82), (exps(2, 0, EXP_UNITS), 0.86, 1.0),
            (pvs(0), 0.73, 0.78), ([("nt", 0)], 0.81, 0.82), (pvs(1), 0.88, 0.94), ([("nt", 1)], 0.97, 0.98),
        ]
    if now and not before:
        woven.append(([("ternary", 1), ("ternary", 2)], 0.9, 1.0))
    steps += weave(*woven)
    steps += if_before(("store",))
    return steps


RING_STEPS = ("tx", "qk", "v", "at", "x1t", "up", "gate", "mt", "nt", "exp", "wsum")


def takes_bank(step):
    return step[0] in RING_STEPS or step[0] == "wo" and step[2] == 0



FIRST, LOOP, LAST = (order_of_steps(True, False), order_of_steps(True, True), order_of_steps(False, True))
RING_FIRST, RING_LOOP = (sum(takes_bank(s) for s in steps) for steps in (FIRST, LOOP))
assert RING_LOOP % RING == 0


def block_kernel(nc, x, w_qkv, b_qkv, b_qkv_cols, w_o, b_o, w_up_t, w_gate_t, w_down_t, k_const, q_const, out, scratch):
    ctx = ExitStack()
    with ctx:
        def sb(name, shape, dt):
            return ctx.enter_context(nc.sbuf_tensor(name, shape, dt))

        def sem(name):
            return ctx.enter_context(nc.semaphore(name))

        wqkv = sb("wqkv", [P, FT, 3 * HID], F32)
        wo = sb("wo_w", [P, FT, HID], F32)
        tern_up = sb("tern_up", [P, FT, EXPERT], F16)
        tern_gate = sb("tern_gate", [P, FT, EXPERT], F16)
        tern_down = sb("tern_down", [P, ET, HID], F16)
        bias_cols = sb("bias_cols", [P, 3 * FT], F32)
        bias_v = sb("bias_v", [P, HID], F32)
        bias_o = sb("bias_o", [P, HID], F32)
        ident = sb("ident", [P, P], F32)
        ident_bf = sb("ident_bf", [P, P], BF16)
        causal = sb("causal", [P, P], BF16)
        ones = sb("ones", [P, P], F32)
        half_neg = sb("half_neg", [P, TT], F32)
        abs_sums = sb("abs_sums", [P, 3], F32)
        scales = sb("scales", [P, 3], F32)
        thresholds = sb("thresholds", [P, 3], F32)
        neg_thresholds = sb("neg_thresholds", [P, 3], F32)
        tanh_scale = sb("tanh_scale", [P, 1], F32)
        ffn_scale = sb("ffn_scale", [P, 1], F32)
        xin = sb("xin", [P, TT, HID], F32)
        x_t = sb("x_t", [P, FT, SEQ], F32)
        qk_rest = sb("qk_rest", [P, QK_TILES, SEQ], F32)
        qk_parts = sb("qk_parts", [P, QK_TILES, 3, SEQ], BF16)
        q_stack = sb("q_stack", [P, HEADS, SEQ], BF16)
        k_stack = sb("k_stack", [P, HEADS, SEQ], BF16)
        neg_max = sb("neg_max", [P, QUADS, P], F32)
        max_parts = sb("max_parts", [P, QUADS, 2, P], BF16)
        probs = sb("probs", [P, 2, EXP_UNITS, SEQ], F32)
        v_ones = sb("v_ones", [P, TT, HEADS, 32], F32)
        pv_t = sb("pv_t", [P, 2, SEQ], F32)
        inv_sum = sb("inv_sum", [P, 2, TT * 4, 1], F32)
        attn = sb("attn", [P, TT, HID], F32)
        attn_t = sb("attn_t", [P, FT, SEQ], F32)
        res = sb("res", [P, TT, HID], F32)
        z = sb("z", [P, TT, HID], F32)
        stats = sb("stats", [P, TT, 6], F32)
        mean_var = sb("mean_var", [P, TT, 2], F32)
        var_eps = sb("var_eps", [P, TT], F32)
        rstd = sb("rstd", [P, TT], F32)
        x1 = sb("x1", [P, TT, HID], F32)
        x1_hi = sb("x1_hi", [P, FT, SEQ], F16)
        x1_lo = sb("x1_lo", [P, FT, SEQ], F16)
        gating = sb("gating", [P, 4, SEQ], F32)
        hidden = sb("hidden", [P, 2, SEQ], F32)
        hidden_hi = sb("hidden_hi", [P, ET, SEQ], F16)
        hidden_lo = sb("hidden_lo", [P, ET, SEQ], F16)
        y = sb("y", [P, TT, HID], F32)
        stage_up = gating[:, :, :].rearrange("p a b -> p (a b)")
        stage_gate = hidden_hi[:, :, :].rearrange("p a b -> p (a b)").bitcast(F32)
        stage_down = hidden_lo[:, :, :].rearrange("p a b -> p (a b)").bitcast(F32)

        ring = [ctx.enter_context(nc.psum_tensor(f"ring{i}", [P, 512], F32)) for i in range(RING)]
        max_bank = [ctx.enter_context(nc.psum_tensor(f"max_bank{i}", [P, 512], F32)) for i in range(2)]
        acc = [ctx.enter_context(nc.psum_tensor(f"acc{i}", [P, 512], F32)) for i in range(2)]

        ring_filled = [sem(f"ring_filled{i}") for i in range(RING)]
        ring_drained = [sem(f"ring_drained{i}") for i in range(RING)]
        max_filled = [sem(f"max_filled{i}") for i in range(2)]
        max_drained = [sem(f"max_drained{i}") for i in range(2)]
        acc_filled = [sem(f"acc_filled{i}") for i in range(2)]
        acc_drained = [sem(f"acc_drained{i}") for i in range(2)]
        weights_in = [sem(f"weights_in{i}") for i in range(4)]
        dve_passed, pool_passed, sp_passed = sem("dve_passed"), sem("pool_passed"), sem("sp_passed")
        consts_set = sem("consts_set")
        dve_consts = sem("dve_consts")
        pool_step = sem("pool_step")
        q_bias_scaled = sem("q_bias_scaled")
        abs_summed = sem("abs_summed")
        quant_step = sem("quant_step")
        ternary_done = sem("ternary_done")
        x_in = sem("x_in")
        res_in = sem("res_in")
        res_biased = sem("res_biased")
        qk_hi_done = sem("qk_hi_done")
        qk_rest_done = [sem(f"qk_rest_done{i}") for i in range(FT)]
        qk_mid_done = [sem(f"qk_mid_done{i}") for i in range(FT)]
        qk_split = [sem(f"qk_split{i}") for i in range(FT)]
        parts_written = [sem(f"parts_written{t}") for t in range(QK_TILES)]
        stack_in = [sem(f"stack_in{i}") for i in range(FT)]
        max_hi_done = sem("max_hi_done")
        max_in = [sem(f"max_in{g}") for g in range(QUADS)]
        masked = sem("masked")
        inverted = sem("inverted")
        stats_done = sem("stats_done")
        moments_done = sem("moments_done")
        var_done = sem("var_done")
        rstd_done = sem("rstd_done")
        x1_done = sem("x1_done")
        x1_hi_done = sem("x1_hi_done")
        tanh_done = sem("tanh_done")
        hidden_hi_done = sem("hidden_hi_done")
        hidden_split = sem("hidden_split")
        y_done = sem("y_done")
        y_stored = sem("y_stored")

        STACK_DMAS = 16 * 2 * len(STACK_RUNS)
        MAX_DMAS = 16 * 2

        def at_least(eng, semaphore, per_batch, batch, k):
            if isinstance(batch, int) and per_batch * batch + k == 0:
                return
            eng.wait_ge(semaphore, batch * per_batch + k)

        class Ring:

            def __init__(self, steps, it):
                self.it = it
                self.at = {s: n for n, s in enumerate(s for s in steps if takes_bank(s))}

            def slot(self, step):
                if isinstance(self.it, int) and self.it == 0:
                    return self.at[step] % RING
                return (RING_FIRST + self.at[step]) % RING

            def bank(self, step):
                return ring[self.slot(step)]

            def fills(self, step):
                if isinstance(self.it, int) and self.it == 0:
                    return self.at[step] // RING
                return self.it * (RING_LOOP // RING) + (
                    (RING_FIRST + self.at[step]) // RING - RING_LOOP // RING)

            def wait_free(self, eng, step):
                n = self.fills(step)
                if not (isinstance(n, int) and n == 0):
                    eng.wait_ge(ring_drained[self.slot(step)], n)

            def wait_filled(self, eng, step):
                eng.wait_ge(ring_filled[self.slot(step)], self.fills(step) + 1)

            def wait_drained(self, eng, step):
                eng.wait_ge(ring_drained[self.slot(step)], self.fills(step) + 1)

            def filled(self, instruction, step):
                instruction.then_inc(ring_filled[self.slot(step)], 1)

            def drained(self, instruction, step):
                instruction.then_inc(ring_drained[self.slot(step)], 1)

        def max_at(g, n):
            u = g * MAX_UNITS + n
            return u % 2, u // 2

        def part_slot(t, part):
            return 2 - part if t % 2 else part

        MAX_PER_BANK = QUADS * MAX_UNITS // 2

        def iterations(eng, body):
            body(FIRST, 0)
            with eng.Fori(1, BATCH) as it:
                body(LOOP, it)
            body(LAST, BATCH)

        block = ctx.enter_context(nc.Block())

        @block.sync
        def _(sp):
            sp.sem_inc(var_done, 2)
            sp.sem_inc(y_stored, 16)
            sp.dma_start(wqkv[:, :, :], w_qkv.rearrange("(t p) n -> p t n", p=P)).then_inc(weights_in[0], 16)
            sp.dma_start(bias_cols[:, :], b_qkv_cols).then_inc(weights_in[0], 16)
            sp.dma_start(bias_v[:, :], b_qkv[2 * HID:3 * HID].unsqueeze(0).broadcast_to([P, HID])).then_inc(weights_in[0], 16)
            sp.dma_start(bias_o[:, :], b_o.unsqueeze(0).broadcast_to([P, HID])).then_inc(weights_in[1], 16)
            sp.dma_start(wo[:, :, :], w_o.rearrange("(t p) n -> p t n", p=P)).then_inc(weights_in[1], 16)
            sp.dma_start(k_stack[DATA_ROWS:P, :, :].bitcast(U16), k_const).then_inc(weights_in[2], 16)
            sp.dma_start(q_stack[DATA_ROWS:P, :, :].bitcast(U16),
                         q_const.unsqueeze(1).broadcast_to([CONST_ROWS, HEADS, SEQ])).then_inc(weights_in[2], 16)

            def sp_at_least(semaphore, per_batch, batch, k):
                at_least(sp, semaphore, per_batch, batch, k)
                sp.sem_inc(sp_passed, 1)

            def body(steps, it):
                rg = Ring(steps, it)
                prev = it - 1
                first = isinstance(it, int) and it == 0
                for step in steps:
                    kind = step[0]
                    if kind == "load_x":
                        sp_at_least(parts_written[0], 16, it, 0)
                        sp.dma_start(xin[:, :, :], x[it].rearrange("(t p) d -> p t d", p=P)).then_inc(x_in, 16)
                        if first:
                            sp.dma_start(stage_up, w_up_t.rearrange("(t p) n -> p t n", p=P)).then_inc(weights_in[3], 16)
                            sp.dma_start(stage_gate, w_gate_t.rearrange("(t p) n -> p t n", p=P)).then_inc(weights_in[3], 16)
                            sp.dma_start(stage_down, w_down_t.rearrange("(t p) n -> p t n", p=P)).then_inc(weights_in[3], 16)
                    elif kind == "load_res":
                        sp_at_least(var_done, 2, it, 0)
                        sp.dma_start(res[:, :, :], x[prev].rearrange("(t p) d -> p t d", p=P)).then_inc(res_in, 16)
                    elif kind == "stack_write":
                        t = step[1]
                        sp_at_least(qk_split[t // 2], 2, it, t % 2 + 1)
                        sp_at_least(stack_in[t // 2], STACK_DMAS, it, 0)
                        sp.dma_start(scratch[t].rearrange("s p n -> p s n"), qk_parts[:, t, :, :]).then_inc(parts_written[t], 16)
                    elif kind == "stack_read":
                        half = step[1]
                        for t, stack in ((2 * half, q_stack), (2 * half + 1, k_stack)):
                            sp_at_least(parts_written[t], 16, it, 16)
                            if not first:
                                sp_at_least(masked, 2 * QUADS, prev, QUADS * (half + 1))
                            row = 0
                            for slot, n in STACK_RUNS:
                                if t % 2 == 1:
                                    slot = 3 - slot - n
                                sp.dma_start(
                                    stack[row:row + DH * n, HEADS // 2 * half:HEADS // 2 * (half + 1), :],
                                    scratch[t, slot:slot + n].rearrange("s (d h) n -> (s d) h n", d=DH),
                                ).then_inc(stack_in[half], 16)
                                row += DH * n
                    elif kind == "mt":
                        g = step[1]
                        rg.wait_drained(sp, step)
                        sp.sem_inc(sp_passed, 1)
                        for part in range(2):
                            sp.dma_start(
                                q_stack[MAX_ROW + part:MAX_ROW + part + 1, 4 * g:4 * g + 4, :],
                                max_parts[0:4 * TT, g, part, :],
                            ).then_inc(max_in[g], 16)
                    elif kind == "store":
                        sp_at_least(y_done, TT, prev, TT)
                        sp.dma_start(out[prev].rearrange("(t p) d -> p t d", p=P), y[:, :, :]).then_inc(y_stored, 16)

            iterations(sp, body)
            sp.wait_ge(y_stored, 16 * (BATCH + 1))
            for t in range(QK_TILES):
                sp.wait_ge(parts_written[t], 16 * BATCH)

        @block.tensor
        def _(pe):
            def body(steps, it):
                rg = Ring(steps, it)
                prev = it - 1
                first = isinstance(it, int) and it == 0
                for step in steps:
                    kind = step[0]
                    if takes_bank(step):
                        rg.wait_free(pe, step)
                        bank = rg.bank(step)
                    if kind == "tx":
                        f = step[1]
                        if f == 0:
                            at_least(pe, x_in, 16, it, 16)
                            if first:
                                pe.wait_ge(consts_set, 1)
                        for t in range(TT):
                            mm = pe.transpose(bank[:, P * t:P * (t + 1)], xin[:, t, P * f:P * (f + 1)], ident[:, :])
                        rg.filled(mm, step)
                    elif kind == "qk":
                        t = step[1]
                        if t == 0:
                            rg.wait_drained(pe, ("tx", 0))
                            rg.wait_drained(pe, ("tx", 1))
                            if first:
                                pe.wait_ge(weights_in[0], 48)
                        col = HID * (t % 2) + P * (t // 2)
                        for f in range(FT):
                            mm = pe.matmul(bank[:, :], wqkv[:, f, col:col + P], x_t[:, f, :], start=(f == 0), stop=(f == FT - 1))
                        rg.filled(mm, step)
                    elif kind == "v":
                        t = step[1]
                        for f in range(FT):
                            mm = pe.matmul(bank[:, 0:HID], x_t[:, f, P * t:P * (t + 1)], wqkv[:, f, 2 * HID:3 * HID],
                                           start=(f == 0), stop=(f == FT - 1))
                        rg.filled(mm, step)
                    elif kind == "max":
                        _, g, n = step
                        k, use = max_at(g, n)
                        if n == 0 and g % 2 == 0:
                            at_least(pe, stack_in[g // 2], STACK_DMAS, it, STACK_DMAS)
                            if first:
                                pe.wait_ge(weights_in[2], 32)
                        at_least(pe, max_drained[k], MAX_PER_BANK, it, use)
                        heads, tile = max_unit(n)
                        width = P * (tile + 1)
                        for i, h in enumerate(heads):
                            o = max_bank[k][:, width * i:width * (i + 1)]
                            pe.matmul(o, q_stack[0:MAX_ROW, 4 * g + h, P * tile:P * (tile + 1)],
                                      k_stack[0:MAX_ROW, 4 * g + h, 0:width], start=True, stop=False)
                            mm = pe.matmul(o[:, width - P:width], ident_bf[:, :], causal[:, :], start=False, stop=True)
                        mm.then_inc(max_filled[k], 1)
                    elif kind == "mt":
                        g = step[1]
                        if first and g == 0:
                            pe.wait_ge(dve_consts, 1)
                        for n in (MAX_UNITS - 2, MAX_UNITS - 1):
                            k, use = max_at(g, n)
                            at_least(pe, max_drained[k], MAX_PER_BANK, it, use + 1)
                        rg.filled(pe.transpose(bank[:, 0:P], neg_max[:, g, :], ident[:, :]), step)
                    elif kind == "exp":
                        _, g, n = step
                        if n == 0:
                            at_least(pe, max_in[g], MAX_DMAS, prev if of_batch_before(step) else it, MAX_DMAS)
                        for h, j, col in exp_unit(n):
                            mm = pe.matmul(bank[:, col:col + SEQ - P * j], k_stack[:, 4 * g + h, P * j:P * (j + 1)],
                                           q_stack[:, 4 * g + h, P * j:SEQ], start=True, stop=True)
                        rg.filled(mm, step)
                    elif kind == "pv":
                        _, g, j = step
                        batch = prev if of_batch_before(step) else it
                        if j == 0:
                            at_least(pe, masked, 2 * QUADS, batch, 2 * (g + 1))
                            at_least(pe, acc_drained[g % 2], 3, batch, g // 2)
                            if g == 0:
                                rg.wait_drained(pe, ("v", TT - 1))
                        for h in range(4):
                            n, col = piece(h, j)
                            mm = pe.matmul(acc[g % 2][32 * h:32 * (h + 1), P * j:SEQ], v_ones[:, j, 4 * g + h, :],
                                           probs[:, g % 2, n, col:col + SEQ - P * j], start=(j == 0), stop=(j == TT - 1))
                        if j == TT - 1:
                            mm.then_inc(acc_filled[g % 2], 1)
                    elif kind == "nt":
                        g = step[1]
                        batch = prev if of_batch_before(step) else it
                        at_least(pe, acc_drained[g % 2], 3, batch, g // 2 + 1)
                        for t in range(TT):
                            mm = pe.transpose(bank[:, P * t:P * (t + 1)], pv_t[:, g % 2, P * t:P * (t + 1)], ident[:, :])
                        rg.filled(mm, step)
                    elif kind == "at":
                        f = step[1]
                        rg.wait_drained(pe, ("nt", 2 + f))
                        for t in range(TT):
                            mm = pe.transpose(bank[:, P * t:P * (t + 1)], attn[:, t, P * f:P * (f + 1)], ident[:, :])
                        rg.filled(mm, step)
                    elif kind == "wo":
                        _, u, f = step
                        bank = rg.bank(("wo", u, 0))
                        if u == 0:
                            rg.wait_drained(pe, ("at", f))
                            pe.wait_ge(weights_in[1], 32)
                        for i in range(2):
                            mm = pe.matmul(bank[:, HID * i:HID * (i + 1)], attn_t[:, f, P * (2 * u + i):P * (2 * u + i + 1)],
                                           wo[:, f, :], start=(f == 0 and i == 0), stop=(f == FT - 1), skip_group_check=True)
                        if f == FT - 1:
                            rg.filled(mm, ("wo", u, 0))
                    elif kind == "x1t":
                        u = step[1]
                        at_least(pe, x1_done, TT, prev, 2 * u + 2)
                        for f in range(FT):
                            for i in range(2):
                                mm = pe.transpose(bank[:, HID * f + P * i:HID * f + P * (i + 1)],
                                                  x1[:, 2 * u + i, P * f:P * (f + 1)], ident[:, :])
                        rg.filled(mm, step)
                    elif kind in ("up", "gate"):
                        m = step[1]
                        w = tern_up if kind == "up" else tern_gate
                        if step == ("up", 0):
                            at_least(pe, x1_hi_done, TT // 2, prev, TT // 2)
                            pe.wait_ge(ternary_done, 3)
                        for part in (x1_hi, x1_lo):
                            if step == ("up", 0) and part is x1_lo:
                                rg.wait_drained(pe, ("x1t", 1))
                            for f in range(FT):
                                mm = pe.matmul(bank[:, :], w[:, f, P * m:P * (m + 1)], part[:, f, :],
                                               start=(f == 0 and part is x1_hi), stop=(f == FT - 1 and part is x1_lo))
                        rg.filled(mm, step)
                    elif kind == "down":
                        m = step[1]
                        if m == 0:
                            for k in range(2):
                                at_least(pe, acc_drained[k], 3, prev, 2)
                        at_least(pe, hidden_split, ET, prev, m + 1)
                        for t in range(TT):
                            for part in (hidden_hi, hidden_lo):
                                mm = pe.matmul(acc[t // 2][:, HID * (t % 2):HID * (t % 2 + 1)], part[:, m, P * t:P * (t + 1)],
                                               tern_down[:, m, :], start=(m == 0 and part is hidden_hi and t % 2 == 0),
                                               stop=(m == ET - 1 and part is hidden_lo), skip_group_check=True)
                            if m == ET - 1 and t % 2 == 1:
                                mm.then_inc(acc_filled[t // 2], 1)
                    elif kind == "wsum":
                        pe.wait_ge(abs_summed, 3)
                        pe.wait_ge(dve_consts, 1)
                        rg.filled(pe.matmul(bank[:, 0:3], ones[:, :], abs_sums[:, :], start=True, stop=True), step)

            iterations(pe, body)

        @block.scalar
        def _(act):
            def body(steps, it):
                rg = Ring(steps, it)
                prev = it - 1
                first = isinstance(it, int) and it == 0
                for step in steps:
                    kind = step[0]
                    if kind == "tx":
                        rg.wait_filled(act, step)
                        rg.drained(act.activation(x_t[:, step[1], :], rg.bank(step)[:, :], ACT.Copy), step)
                    elif kind == "qk":
                        t = step[1]
                        if first and t == 0:
                            act.wait_ge(q_bias_scaled, 1)
                        scale = DH ** -0.5 if t % 2 == 0 else 1.0
                        bias = bias_cols[:, FT * (t % 2) + t // 2:FT * (t % 2) + t // 2 + 1]
                        at_least(act, parts_written[t], 16, it, 0)
                        hi = qk_parts[:, t, part_slot(t, 0), :]
                        if t < 2:
                            rg.wait_drained(act, step)
                            act.activation(hi, qk_rest[:, t, :], ACT.Copy).then_inc(qk_hi_done, 1)
                        else:
                            rg.wait_filled(act, step)
                            act.activation(hi, rg.bank(step)[:, :], ACT.Identity, bias=bias, scale=scale)
                            rg.drained(act.activation(qk_rest[:, t, :], rg.bank(step)[:, :], ACT.Identity, bias=bias,
                                                      scale=scale), step)
                    elif kind == "exp":
                        _, g, n = step
                        if n == 0 and not (first and g < 2):
                            at_least(act, acc_filled[g % 2], 3, it if g == 2 else prev, 1 if g >= 2 else 2)
                        rg.wait_filled(act, step)
                        rg.drained(act.activation(probs[:, g % 2, n, :], rg.bank(step)[:, :], ACT.Exp), step)
                    elif kind == "pv" and step[2] == TT - 1:
                        g = step[1]
                        batch = prev if of_batch_before(step) else it
                        at_least(act, acc_filled[g % 2], 3, batch, g // 2 + 1)
                        act.activation(pv_t[:, g % 2, :], acc[g % 2][:, :], ACT.Copy).then_inc(acc_drained[g % 2], 1)
                    elif kind == "at":
                        rg.wait_filled(act, step)
                        rg.drained(act.activation(attn_t[:, step[1], :], rg.bank(step)[:, :], ACT.Copy), step)
                    elif kind == "x1t":
                        u = step[1]
                        rg.wait_filled(act, step)
                        act.activation(x1_hi[:, :, 2 * P * u:2 * P * (u + 1)],
                                       rg.bank(step)[:, :].rearrange("p (f n) -> p f n", f=FT), ACT.Copy).then_inc(x1_hi_done, 1)
                    elif kind == "up":
                        m = step[1]
                        if m >= 2:
                            rg.wait_drained(act, ("up", m - 2))
                        rg.wait_filled(act, step)
                        act.activation(gating[:, m % 2, :], rg.bank(step)[:, :], ACT.Tanh,
                                       scale=tanh_scale[:, 0:1]).then_inc(tanh_done, 1)
                    elif kind == "hidden_hi":
                        m = step[1]
                        rg.wait_drained(act, ("gate", m))
                        act.activation(hidden_hi[:, m, :], hidden[:, m % 2, :], ACT.Copy).then_inc(hidden_hi_done, 1)

            iterations(act, body)

        @block.vector
        def _(dve):
            dve.memset(ones[:, :], 1.0)
            dve.memset(half_neg[:, :], -0.5)
            dve.memset(neg_max[:, :, :], 0.0)
            dve.memset(v_ones[:, :, :, :], 1.0).then_inc(dve_consts, 1)
            dve.wait_ge(dve_consts, 1)
            dve.wait_ge(weights_in[0], 48)
            dve.tensor_scalar(bias_cols[:, 0:FT], bias_cols[:, 0:FT], DH ** -0.5, None, ALU.mult).then_inc(q_bias_scaled, 1)
            dve.wait_ge(q_bias_scaled, 1)

            def normalise(batch, which, target, done):
                at_least(dve, rstd_done, 2, batch, which + 1)
                for t in range(TT):
                    dve.tensor_scalar(target[:, t, :], z[:, t, :], mean_var[:, t, 0:1], rstd[:, t:t + 1],
                                      ALU.subtract, ALU.mult).then_inc(done, 1)

            def variances(batch, which):
                at_least(dve, moments_done, 2 * TT, batch, (which + 1) * TT)
                dve.tensor_scalar(var_eps[:, :], mean_var[:, :, 1], LN_EPS, None, ALU.add).then_inc(var_done, 1)

            def body(steps, it):
                rg = Ring(steps, it)
                prev = it - 1
                first = isinstance(it, int) and it == 0
                for step in steps:
                    kind = step[0]
                    if kind == "split" and step[1] < 2:
                        t = step[1]
                        hi, mid, lo = [qk_parts[:, t, part_slot(t, part), :] for part in range(3)]
                        bias = bias_cols[:, FT * (t % 2):FT * (t % 2) + 1]
                        rg.wait_filled(dve, ("qk", t))
                        rg.drained(dve.tensor_scalar(qk_rest[:, t, :], rg.bank(("qk", t))[:, :], DH ** -0.5 if t == 0 else 1.0,
                                                     bias, ALU.mult, ALU.add), ("qk", t))
                        at_least(dve, qk_hi_done, 2, it, t + 1)
                        dve.tensor_tensor(qk_rest[:, t, :], qk_rest[:, t, :], hi, ALU.subtract).then_inc(qk_rest_done[0], 1)
                        at_least(dve, qk_rest_done[0], 2, it, t + 1)
                        dve.tensor_copy(mid, qk_rest[:, t, :]).then_inc(qk_mid_done[0], 1)
                        at_least(dve, qk_mid_done[0], 2, it, t + 1)
                        dve.tensor_tensor(lo, qk_rest[:, t, :], mid, ALU.subtract).then_inc(qk_split[0], 1)
                    elif kind == "v_out":
                        v = ("v", step[1])
                        rg.wait_filled(dve, v)
                        rg.drained(dve.tensor_tensor(
                            v_ones[:, step[1], :, 0:DH], rg.bank(v)[:, 0:HID].rearrange("p (h d) -> p h d", d=DH),
                            bias_v[:, :].rearrange("p (h d) -> p h d", d=DH), ALU.add), v)
                    elif kind == "take":
                        _, g, n = step
                        k, use = max_at(g, n)
                        heads, tile = max_unit(n)
                        width = P * (tile + 1)
                        at_least(dve, max_filled[k], MAX_PER_BANK, it, use + 1)
                        first_col = 4 * heads[0] + tile
                        dve.tensor_reduce(
                            neg_max[:, g, first_col:first_col + 4 * (len(heads) - 1) + 1:4],
                            max_bank[k][:, 0:width * len(heads)].rearrange("p (h j) -> p h j", j=width),
                            AX_X, ALU.max, negate=True).then_inc(max_drained[k], 1)
                    elif kind == "mt":
                        g = step[1]
                        at_least(dve, max_in[g], MAX_DMAS, it, 0)
                        rg.wait_filled(dve, step)
                        m_t = rg.bank(step)[0:4 * TT, 0:P]
                        dve.tensor_copy(max_parts[0:4 * TT, g, 0, :], m_t).then_inc(max_hi_done, 1)
                        at_least(dve, max_hi_done, QUADS, it, g + 1)
                        rg.drained(dve.tensor_tensor(max_parts[0:4 * TT, g, 1, :], m_t, max_parts[0:4 * TT, g, 0, :],
                                                     ALU.subtract), step)
                    elif kind == "nt":
                        g = step[1]
                        batch = prev if of_batch_before(step) else it
                        rg.wait_filled(dve, step)
                        heads = rg.bank(step)[:, :].rearrange("p (s c) -> p s c", c=32)
                        dve.reciprocal(inv_sum[:, g % 2, :, :], heads[:, :, DH:DH + 1]).then_inc(inverted, 1)
                        at_least(dve, inverted, QUADS, batch, g + 1)
                        rg.drained(dve.tensor_tensor(
                            attn[:, :, 4 * DH * g:4 * DH * (g + 1)].rearrange("p t (h d) -> p t h d", d=DH),
                            heads[:, :, 0:DH].rearrange("p (t h) d -> p t h d", t=TT),
                            inv_sum[:, g % 2, :, :].rearrange("p (t h) o -> p t h o", t=TT).broadcast_to([P, TT, 4, DH]),
                            ALU.mult), step)
                    elif kind == "wo" and step[2] == FT - 1:
                        u = step[1]
                        bank = ("wo", u, 0)
                        if u == 0:
                            at_least(dve, res_biased, 1, prev, 1)
                        rg.wait_filled(dve, bank)
                        rg.drained(dve.tensor_tensor(
                            z[:, 2 * u:2 * u + 2, :], rg.bank(bank)[:, :].rearrange("p (t d) -> p t d", d=HID),
                            res[:, 2 * u:2 * u + 2, :], ALU.add), bank)
                        rg.wait_drained(dve, bank)
                        for t in (2 * u, 2 * u + 1):
                            dve.bn_stats(stats[:, t, :], z[:, t, :]).then_inc(stats_done, 1)
                        for t in (2 * u, 2 * u + 1):
                            at_least(dve, stats_done, 2 * TT, prev, t + 1)
                            dve.sem_inc(dve_passed, 1)
                            dve.bn_aggr(mean_var[:, t, :], stats[:, t, :]).then_inc(moments_done, 1)
                        if u == 1:
                            variances(prev, 0)
                    elif kind == "ln1":
                        normalise(prev, 0, x1, x1_done)
                    elif kind == "x1_lo":
                        u = step[1]
                        x1t = ("x1t", u)
                        tokens = slice(2 * P * u, 2 * P * (u + 1))
                        at_least(dve, x1_hi_done, TT // 2, prev, u + 1)
                        rg.drained(dve.tensor_tensor(x1_lo[:, :, tokens], rg.bank(x1t)[:, :].rearrange("p (f n) -> p f n", f=FT),
                                                     x1_hi[:, :, tokens], ALU.subtract), x1t)
                    elif kind == "swish":
                        m = step[1]
                        up = ("up", m)
                        at_least(dve, tanh_done, ET, prev, m + 1)
                        rg.drained(dve.scalar_tensor_tensor(
                            out=gating[:, 2 + m % 2, :], in0=gating[:, m % 2, :], scalar=1.0, in1=rg.bank(up)[:, :],
                            op0=ALU.add, op1=ALU.mult), up)
                    elif kind == "swiglu":
                        m = step[1]
                        up, gate = ("up", m), ("gate", m)
                        if m >= 2:
                            at_least(dve, hidden_split, ET, prev, m - 1)
                        rg.wait_filled(dve, gate)
                        rg.wait_drained(dve, up)
                        rg.drained(dve.scalar_tensor_tensor(
                            out=hidden[:, m % 2, :], in0=gating[:, 2 + m % 2, :], scalar=HIDDEN_SCALE,
                            in1=rg.bank(gate)[:, :], op0=ALU.mult, op1=ALU.mult), gate)
                    elif kind == "ffn_sum":
                        u = step[1]
                        at_least(dve, acc_filled[u], 3, prev, 3)
                        dve.scalar_tensor_tensor(
                            out=z[:, 2 * u:2 * u + 2, :].rearrange("p t d -> p (t d)"), in0=acc[u][:, :], scalar=ffn_scale[:, 0:1],
                            in1=x1[:, 2 * u:2 * u + 2, :].rearrange("p t d -> p (t d)"), op0=ALU.mult, op1=ALU.add,
                        ).then_inc(acc_drained[u], 1)
                    elif kind == "ffn_stats":
                        t = step[1]
                        if t % 2 == 0:
                            at_least(dve, acc_drained[t // 2], 3, prev, 3)
                        dve.bn_stats(stats[:, t, :], z[:, t, :]).then_inc(stats_done, 1)
                        at_least(dve, stats_done, 2 * TT, prev, TT + t + 1)
                        dve.sem_inc(dve_passed, 1)
                        dve.bn_aggr(mean_var[:, t, :], stats[:, t, :]).then_inc(moments_done, 1)
                        if t == TT - 1:
                            variances(prev, 1)
                    elif kind == "ln2":
                        at_least(dve, y_stored, 16, it, 0)
                        normalise(prev, 1, y, y_done)
                    elif kind == "abs_sums":
                        dve.wait_ge(weights_in[3], 48)
                        for i, w in enumerate((stage_up, stage_gate, stage_down)):
                            dve.tensor_reduce(abs_sums[:, i:i + 1], w, AX_X, ALU.add,
                                              apply_absolute_value=True).then_inc(abs_summed, 1)
                    elif kind == "wsum":
                        rg.wait_filled(dve, step)
                        rg.drained(dve.tensor_scalar(scales[:, :], rg.bank(step)[:, 0:3], 1.0 / (EXPERT * HID), QUANT_EPS,
                                                     ALU.mult, ALU.add), step)
                        rg.wait_drained(dve, step)
                        dve.tensor_scalar(thresholds[:, :], scales[:, :], 0.5, None, ALU.mult).then_inc(quant_step, 1)
                        dve.tensor_scalar(neg_thresholds[:, :], scales[:, :], -0.5, None, ALU.mult).then_inc(quant_step, 1)
                        dve.tensor_scalar(tanh_scale[:, :], scales[:, 0:1], 0.5, None, ALU.mult).then_inc(quant_step, 1)
                        dve.tensor_scalar(ffn_scale[:, :], scales[:, 1:2], scales[:, 2:3], 1.0 / HIDDEN_SCALE,
                                          ALU.mult, ALU.mult).then_inc(quant_step, 1)
                        dve.wait_ge(quant_step, 4)
                        dve.tensor_tensor(ffn_scale[:, :], ffn_scale[:, :], tanh_scale[:, :], ALU.mult).then_inc(quant_step, 1)
                    elif kind == "ternary":
                        i = step[1]
                        w = (stage_up, stage_gate, stage_down)[i]
                        t = (tern_up, tern_gate, tern_down)[i][:, :, :].rearrange("p a b -> p (a b)")
                        dve.tensor_scalar(t, w, neg_thresholds[:, i:i + 1], None, ALU.is_lt).then_inc(quant_step, 1)
                        dve.wait_ge(quant_step, 6 + i)
                        dve.scalar_tensor_tensor(out=t, in0=w, scalar=thresholds[:, i:i + 1], in1=t,
                                                 op0=ALU.is_gt, op1=ALU.subtract).then_inc(ternary_done, 1)

            iterations(dve, body)

        @block.gpsimd
        def _(pool):
            pool.memset(ident[:, :], 0.0).then_inc(pool_step, 1)
            pool.memset(causal[:, :], 0.0).then_inc(pool_step, 1)
            pool.wait_ge(pool_step, 2)
            pool.affine_select(out=ident[:, :], in_=ident[:, :], compare_op=ALU.not_equal, fill=1.0, base=0,
                               pattern=[[-1, P]], channel_multiplier=1).then_inc(pool_step, 1)
            pool.affine_select(out=causal[:, :], in_=causal[:, :], compare_op=ALU.is_ge, fill=MASKED, base=0,
                               pattern=[[-1, P]], channel_multiplier=1).then_inc(pool_step, 1)
            pool.wait_ge(pool_step, 4)
            pool.tensor_copy(ident_bf[:, :], ident[:, :]).then_inc(consts_set, 1)
            pool.wait_ge(dve_consts, 1)

            def keep_past(v, blocks):
                return pool.affine_select(out=v, in_=v, compare_op=ALU.is_ge, fill=0.0, base=0,
                                          pattern=([[0, blocks]] if blocks > 1 else []) + [[1, P]], channel_multiplier=-1)

            def body(steps, it):
                rg = Ring(steps, it)
                prev = it - 1
                for step in steps:
                    kind = step[0]
                    if kind == "load_res":
                        at_least(pool, res_in, 16, prev, 16)
                        pool.wait_ge(weights_in[1], 32)
                        for t in range(TT):
                            ins = pool.tensor_tensor(res[:, t, :], res[:, t, :], bias_o[:, :], ALU.add)
                        ins.then_inc(res_biased, 1)
                    elif kind == "split" and step[1] >= 2:
                        t = step[1]
                        hi, mid, lo = [qk_parts[:, t, part_slot(t, part), :] for part in range(3)]
                        rg.wait_drained(pool, ("qk", t))
                        pool.tensor_tensor(qk_rest[:, t, :], qk_rest[:, t, :], hi, ALU.subtract).then_inc(qk_rest_done[1], 1)
                        at_least(pool, qk_rest_done[1], 2, it, t - 1)
                        pool.sem_inc(pool_passed, 1)
                        pool.tensor_copy(mid, qk_rest[:, t, :]).then_inc(qk_mid_done[1], 1)
                        at_least(pool, qk_mid_done[1], 2, it, t - 1)
                        pool.tensor_tensor(lo, qk_rest[:, t, :], mid, ALU.subtract).then_inc(qk_split[1], 1)
                    elif kind in ("ln1", "ln2"):
                        at_least(pool, var_done, 2, it, 1 if kind == "ln1" else 2)
                        pool.tensor_tensor(rstd[:, :], var_eps[:, :], half_neg[:, :], ALU.pow).then_inc(rstd_done, 1)
                    elif kind == "hidden_hi":
                        m = step[1]
                        at_least(pool, hidden_hi_done, ET, prev, m + 1)
                        pool.tensor_tensor(hidden_lo[:, m, :], hidden[:, m % 2, :], hidden_hi[:, m, :],
                                           ALU.subtract).then_inc(hidden_split, 1)
                    elif kind == "exp" and step[2] % 5 in (1, 3, 4):
                        _, g, n = step
                        rg.wait_drained(pool, step)
                        pool.sem_inc(pool_passed, 1)
                        if n % 5 == 4:
                            both = probs[:, g % 2, n, :].rearrange("p (h q) -> p h q", h=2)
                            keep_past(both[:, :, 0:P], 2).then_inc(masked, 1)
                        else:
                            keep_past(probs[:, g % 2, n - 1:n + 1, 0:P], 2)
                            keep_past(probs[:, g % 2, n, P:2 * P], 1)

            iterations(pool, body)


def bf16_parts(values):
    parts = []
    for _ in range(3):
        bits = values.view(np.uint32) & np.uint32(0xFFFF0000)
        parts.append((bits >> np.uint32(16)).astype(np.uint16))
        values = values - bits.view(np.float32)
    return parts


def constant_rows():
    one, masked = 0x3F80, bf16_parts(np.asarray([MASKED], np.float32))[0][0]
    slopes = np.asarray([1.0 / 2 ** (k / 2) for k in range(HEADS)], np.float32)
    position = np.arange(SEQ)
    k_rows = np.zeros((CONST_ROWS, HEADS, SEQ), np.uint16)
    q_rows = np.zeros((CONST_ROWS, SEQ), np.uint16)
    k_rows[0:3] = bf16_parts(slopes[:, None] * position.astype(np.float32)[None, :])
    q_rows[0:3] = one
    for group in range(MAX_ROW - DATA_ROWS - 3):
        q_rows[3 + group, position // GROUP == group] = one
        k_rows[3 + group, :, position // GROUP > group] = masked
    k_rows[MAX_ROW - DATA_ROWS:MAX_ROW - DATA_ROWS + 2] = one
    return k_rows, q_rows


def kernel(L0_attn_x, L0_attn_Wqkv, L0_attn_bqkv, L0_attn_Wo, L0_attn_bo, L0_ffn_W_up, L0_ffn_W_gate, L0_ffn_W_down):
    import concourse.bacc as bacc
    from concourse.bass_utils import run_bass_kernel_spmd

    def by_dimension(a):
        a = np.array(a)
        qk = a[..., :2 * HID].reshape(a.shape[:-1] + (QK_TILES, HEADS // 2, DH))
        a[..., :2 * HID] = np.swapaxes(qk, -1, -2).reshape(a.shape[:-1] + (2 * HID,))
        return a

    k_rows, q_rows = constant_rows()
    w_qkv, b_qkv = by_dimension(L0_attn_Wqkv), by_dimension(L0_attn_bqkv)
    arrays = {
        "x_dram": np.ascontiguousarray(L0_attn_x),
        "w_qkv_dram": w_qkv,
        "b_qkv_dram": b_qkv,
        "b_qkv_cols_dram": np.ascontiguousarray(b_qkv.reshape(3 * FT, P).T),
        "w_o_dram": np.ascontiguousarray(L0_attn_Wo),
        "b_o_dram": np.ascontiguousarray(L0_attn_bo),
        "w_up_dram": np.ascontiguousarray(np.asarray(L0_ffn_W_up).T),
        "w_gate_dram": np.ascontiguousarray(np.asarray(L0_ffn_W_gate).T),
        "w_down_dram": np.ascontiguousarray(np.asarray(L0_ffn_W_down).T),
        "k_const_dram": k_rows,
        "q_const_dram": q_rows,
    }
    nc = bacc.Bacc("TRN2", target_bir_lowering=False, num_devices=1)
    args = [nc.dram_tensor(name, a.shape, mybir.dt.from_np(a.dtype), kind="ExternalInput").ap() for name, a in arrays.items()]
    out = nc.dram_tensor("out_dram", (BATCH, SEQ, HID), F32, kind="ExternalOutput").ap()
    scratch = nc.dram_tensor("qk_scratch", (QK_TILES, 3, P, SEQ), BF16, kind="Internal").ap()
    block_kernel(nc, *args, out, scratch)
    r = run_bass_kernel_spmd(nc, [arrays], core_ids=[0])
    return r.results[0]["out_dram"]
```

```python
from contextlib import ExitStack

import numpy as np

import concourse.bass as bass
from concourse import mybir

F32 = mybir.dt.float32
F16 = mybir.dt.float16
BF16 = mybir.dt.bfloat16
U16 = mybir.dt.uint16
ALU = mybir.AluOpType
ACT = mybir.ActivationFunctionType
AX_X = mybir.AxisListType.X

P = 128
BATCH, SEQ, HID = 8, 512, 256
HEADS = 16
DH = HID // HEADS
EXPERT = 1024
TT = SEQ // P
FT = HID // P
ET = EXPERT // P
QUADS = HEADS // 4
QK_TILES = 2 * FT
LN_EPS = 1e-5
QUANT_EPS = 1e-8
MASKED = -1e30
HIDDEN_SCALE = 0.25

STACK_RUNS = [(0, 3), (0, 2), (0, 1)]
DATA_ROWS = DH * sum(n for _, n in STACK_RUNS)
MAX_ROW = 112
CONST_ROWS = P - DATA_ROWS
GROUP = 40

RING = 4
EXP_UNITS = 10
MAX_UNITS = 11


def max_unit(n):
    if n == 0:
        return [0, 1, 2, 3], 0
    if n < 3:
        return [2 * (n - 1), 2 * (n - 1) + 1], 1
    return ([n - 3], 2) if n < 7 else ([n - 7], 3)


def exp_unit(n):
    pair, k = divmod(n, 5)
    if k == 4:
        return [(2 * pair, 2, 0), (2 * pair + 1, 2, 256)]
    head = 2 * pair + k // 2
    return [(head, 0, 0)] if k % 2 == 0 else [(head, 3, 0), (head, 1, 128)]


def piece(head, key_tile):
    for n in range(EXP_UNITS):
        for h, j, col in exp_unit(n):
            if (h, j) == (head, key_tile):
                return n, col


def weave(*parts):
    keyed = []
    for p, (steps, lo, hi) in enumerate(parts):
        keyed += [(lo + (hi - lo) * (i + 0.5) / len(steps), p, i, s) for i, s in enumerate(steps)]
    return [s for *_, s in sorted(keyed, key=lambda x: x[:3])]


def of_batch_before(step):
    return step[0] == "exp" and step[1] == 3 or step[0] in ("pv", "nt", "nt_out") and step[1] >= 2


def order_of_steps(now, before):
    def if_now(*s):
        return list(s) if now else []

    def if_before(*s):
        return list(s) if before else []

    def exps(g, lo, hi):
        return [("exp", g, n) for n in range(lo, hi)]

    def pvs(g):
        return [("pv", g, j) for j in range(TT)]

    def take_max(units):
        return [s for u in units for s in ([u, ("take", *u[1:])] if u[0] == "max" else [u])]

    steps = if_before(("load_res",))
    steps += if_now(("tx", 0), ("tx", 1), ("qk", 0), ("qk_out", 0), ("split", 0), ("stack_write", 0), ("load_next",))
    steps += if_before(("pv", 2, 0), *exps(3, 0, 2), ("pv", 2, 1), *exps(3, 2, 4))
    steps += if_now(("qk", 1), ("qk_out", 1)) + if_before(("exp", 3, 4), ("pv", 2, 2), ("pv", 2, 3))
    steps += if_now(("split", 1), ("stack_write", 1), ("stack_read", 0))
    steps += if_before(*exps(3, 5, 9), ("nt", 2), ("exp", 3, 9), ("nt_out", 2))
    steps += if_now(("qk", 2), ("split", 2))
    steps += if_before(("at", 0), *pvs(3))
    steps += if_now(("v", 0), ("v_out", 0), ("v", 1), ("v_out", 1), ("stack_write", 2))
    steps += if_before(("nt", 3), ("nt_out", 3), ("wo", 0, 0), ("at", 1), ("wo", 1, 0), ("wo", 0, 1), ("wo", 1, 1))
    if before and now:
        steps += [("max", 0, 0), ("max", 0, 1), ("take", 0, 0), ("v", 2), ("v_out", 2), ("v", 3), ("v_out", 3), ("ln1",),
                  ("qk", 3), ("max", 0, 2), ("x1t", 0), ("x1t", 1), ("take", 0, 1), ("max", 0, 3),
                  ("x1_lo", 0), ("x1_lo", 1), ("take", 0, 2), ("take", 0, 3), ("split", 3)]
    elif now:
        steps += [("v", 2), ("v_out", 2), ("v", 3), ("v_out", 3), ("qk", 3), ("split", 3)]
    else:
        steps += [("ln1",), ("x1t", 0), ("x1t", 1), ("x1_lo", 0), ("x1_lo", 1)]

    maxima = []
    for g in range(QUADS):
        maxima += [("max", g, n) for n in range(4 if before and g == 0 else 0, MAX_UNITS)]
        if g:
            maxima.insert(-MAX_UNITS + 3, ("mt", g - 1))
            maxima.insert(-MAX_UNITS + 4, ("mt_out", g - 1))
    early = maxima.index(("mt_out", 1)) + 1
    ffn = []
    for m in range(ET):
        ffn += [("up", m)] + [("hidden_hi", m - 1)] * (m > 0) + [("gate", m), ("swish", m)]
        ffn += [("down", m - 2)] * (m > 1) + [("swiglu", m)]
    ffn += [("hidden_hi", ET - 1), ("down", ET - 2)]
    woven = []
    if before:
        woven += [
            (ffn, 0.0, 0.6), ([("down", ET - 1)], 0.64, 0.65),
            ([("ln2",)], 0.99, 0.999),
        ]
        woven += [([("ffn_sum", 0)], 0.66, 0.67), ([("ffn_stats", 0)], 0.78, 0.79)] if now else [
            ([("ffn_sum", 0), ("ffn_stats", 0)], 0.66, 0.68)]
        woven += [([("ffn_sum", 1)], 0.71, 0.72), ([("ffn_stats", 1)], 0.92, 0.93)]
    if now:
        woven += [
            ([("stack_write", 3), ("stack_read", 1)], 0.05, 0.07),
            (take_max(maxima[:early]), 0.0, 0.62), (take_max(maxima[early:]), 0.62, 0.91), ([("mt", 3), ("mt_out", 3)], 0.92, 0.95),
            (exps(0, 0, EXP_UNITS), 0.42, 0.64), (exps(1, 0, EXP_UNITS), 0.71, 0.83), (exps(2, 0, EXP_UNITS), 0.88, 1.0),
            (pvs(0), 0.74, 0.79), ([("nt", 0), ("nt_out", 0)], 0.81, 0.85), (pvs(1), 0.88, 0.94), ([("nt", 1), ("nt_out", 1)], 0.955, 0.985),
        ]
    if now and not before:
        woven += [
            ([("abs_sum", i) for i in range(3)], 0.28, 0.36), ([("wsum",)], 0.4, 0.41),
            ([("ternary", 2, 0)], 0.45, 0.46), ([("ternary", 2, 1)], 0.66, 0.67), ([("ternary", 2, 2)], 0.84, 0.85),
            ([("ternary", 0), ("ternary", 1)], 0.94, 0.999),
        ]
    steps += weave(*woven)
    steps += if_before(("store",))
    return steps


RING_STEPS = ("tx", "qk", "v", "at", "x1t", "up", "gate", "mt", "nt", "exp", "wsum")


def takes_bank(step):
    return step[0] in RING_STEPS or step[0] == "wo" and step[2] == 0



LOOP_ORDER = """
    tx.0 tx.1 exp.3.0 exp.3.1 exp.3.2 pv.2.0 exp.3.3 qk.0 qk_out.0 exp.3.4 exp.3.5 qk.1 pv.2.1 split.0 pv.2.2 load_res
    stack_write.0 load_next qk_out.1 exp.3.6 exp.3.7 pv.2.3 exp.3.8 exp.3.9 qk.2 split.1 nt.2 pv.3.0 stack_write.1 pv.3.1
    pv.3.2 stack_read.0 nt_out.2 pv.3.3 at.0 v.0 nt.3 v_out.0 v.1 nt_out.3 wo.0.0 at.1 split.2 wo.1.0 stack_write.2 v_out.1
    wo.0.1 wo.1.1 qk.3 max.0.0 take.0.0 max.0.1 take.0.1 max.0.2 v.2 max.0.3 ln1 x1t.0 take.0.2 take.0.3 x1t.1 v.3 max.0.4
    split.3 v_out.2 x1_lo.0 x1_lo.1 max.0.5 up.0 take.0.4 take.0.5 max.0.6 take.0.6 gate.0 max.0.7 max.0.8 swish.0 v_out.3
    take.0.7 up.1 max.0.9 gate.1 take.0.8 take.0.9 max.0.10 swiglu.0 max.1.0 up.2 take.0.10 hidden_hi.0 max.1.1
    stack_write.3 swish.1 gate.2 up.3 take.1.0 swiglu.1 swish.2 mt.0 take.1.1 max.1.2 gate.3 swiglu.2 max.1.3 take.1.2
    swish.3 take.1.3 hidden_hi.1 down.0 max.1.4 up.4 max.1.5 stack_read.1 hidden_hi.2 take.1.4 mt_out.0 max.1.6 take.1.5
    gate.4 max.1.7 take.1.6 up.5 max.1.8 swiglu.3 gate.5 swish.4 take.1.7 take.1.8 max.1.9 swiglu.4 down.1 take.1.9
    hidden_hi.3 hidden_hi.4 swish.5 max.1.10 max.2.0 up.6 take.1.10 take.2.0 max.2.1 exp.0.0 swiglu.5 gate.6 exp.0.1 swish.6
    swiglu.6 down.2 take.2.1 max.2.2 hidden_hi.5 exp.0.2 up.7 take.2.2 max.2.3 mt.1 swish.7 max.2.4 take.2.3 gate.7 down.3
    max.2.5 down.4 hidden_hi.6 take.2.4 take.2.5 mt_out.1 max.2.6 take.2.6 swiglu.7 exp.0.3 exp.0.4 hidden_hi.7 max.2.7
    exp.0.5 down.5 take.2.7 max.2.8 exp.0.6 down.6 exp.0.7 max.2.9 take.2.8 max.2.10 exp.0.8 down.7 take.2.9 take.2.10
    exp.0.9 max.3.0 exp.1.0 max.3.1 exp.1.1 ffn_sum.0 take.3.0 exp.1.2 max.3.2 exp.1.3 mt.2 ffn_sum.1 take.3.1 take.3.2
    exp.1.4 pv.0.0 max.3.3 mt_out.2 max.3.4 take.3.3 take.3.4 exp.1.5 pv.0.1 ffn_stats.0 exp.1.6 max.3.5 exp.1.7 pv.0.2
    take.3.5 exp.1.8 pv.0.3 max.3.6 exp.1.9 exp.2.0 exp.2.1 max.3.7 ffn_stats.1 nt.0 take.3.6 take.3.7 max.3.8 exp.2.2
    exp.2.3 nt_out.0 max.3.9 take.3.8 pv.1.0 max.3.10 take.3.9 take.3.10 exp.2.4 exp.2.5 exp.2.6 exp.2.7 mt.3 pv.1.1 pv.1.2
    pv.1.3 exp.2.8 mt_out.3 exp.2.9 ln2 nt.1 nt_out.1 store
"""
FIRST, LAST = order_of_steps(True, False), order_of_steps(False, True)
LOOP = [(name, *map(int, numbers)) for name, *numbers in (word.split(".") for word in LOOP_ORDER.split())]
assert sorted(LOOP) == sorted(order_of_steps(True, True))
RING_FIRST, RING_LOOP = (sum(takes_bank(s) for s in steps) for steps in (FIRST, LOOP))
assert RING_LOOP % RING == 0


def block_kernel(nc, x, w_qkv, b_qkv, b_qkv_cols, w_o, b_o, w_up_t, w_gate_t, w_down_t, k_const, q_const, out, scratch):
    ctx = ExitStack()
    with ctx:
        def sb(name, shape, dt):
            return ctx.enter_context(nc.sbuf_tensor(name, shape, dt))

        def sem(name):
            return ctx.enter_context(nc.semaphore(name))

        wqkv = sb("wqkv", [P, FT, 3 * HID], F32)
        wo = sb("wo_w", [P, FT, HID], F32)
        tern_up = sb("tern_up", [P, FT, EXPERT], F16)
        tern_gate = sb("tern_gate", [P, FT, EXPERT], F16)
        tern_down = sb("tern_down", [P, ET, HID], F16)
        bias_cols = sb("bias_cols", [P, 3 * FT], F32)
        bias_v = sb("bias_v", [P, HID], F32)
        bias_o = sb("bias_o", [P, HID], F32)
        ident = sb("ident", [P, P], F32)
        ident_bf = sb("ident_bf", [P, P], BF16)
        causal = sb("causal", [P, P], BF16)
        ones = sb("ones", [P, P], F32)
        half_neg = sb("half_neg", [P, TT], F32)
        abs_sums = sb("abs_sums", [P, 3], F32)
        scales = sb("scales", [P, 3], F32)
        thresholds = sb("thresholds", [P, 3], F32)
        neg_thresholds = sb("neg_thresholds", [P, 3], F32)
        tanh_scale = sb("tanh_scale", [P, 1], F32)
        ffn_scale = sb("ffn_scale", [P, 1], F32)
        xin = sb("xin", [P, TT, HID], F32)
        x_t = sb("x_t", [P, FT, SEQ], F32)
        qk_rest = sb("qk_rest", [P, QK_TILES, SEQ], F32)
        qk_parts = sb("qk_parts", [P, QK_TILES, 3, SEQ], BF16)
        q_stack = sb("q_stack", [P, HEADS, SEQ], BF16)
        k_stack = sb("k_stack", [P, HEADS, SEQ], BF16)
        neg_max = sb("neg_max", [P, QUADS, P], F32)
        max_parts = sb("max_parts", [P, QUADS, 2, P], BF16)
        probs = sb("probs", [P, 2, EXP_UNITS, SEQ], F32)
        v_ones = sb("v_ones", [P, TT, HEADS, 32], F32)
        pv_t = sb("pv_t", [P, 2, SEQ], F32)
        inv_sum = sb("inv_sum", [P, 2, TT * 4, 1], F32)
        attn = sb("attn", [P, TT, HID], F32)
        attn_t = sb("attn_t", [P, FT, SEQ], F32)
        res = sb("res", [P, TT, HID], F32)
        z = sb("z", [P, TT, HID], F32)
        stats = sb("stats", [P, TT, 6], F32)
        mean_var = sb("mean_var", [P, TT, 2], F32)
        var_eps = sb("var_eps", [P, TT], F32)
        rstd = sb("rstd", [P, TT], F32)
        x1 = sb("x1", [P, TT, HID], F32)
        x1_hi = sb("x1_hi", [P, FT, SEQ], F16)
        x1_lo = sb("x1_lo", [P, FT, SEQ], F16)
        gating = sb("gating", [P, 4, SEQ], F32)
        hidden = sb("hidden", [P, 2, SEQ], F32)
        hidden_hi = sb("hidden_hi", [P, ET, SEQ], F16)
        hidden_lo = sb("hidden_lo", [P, ET, SEQ], F16)
        y = sb("y", [P, TT, HID], F32)
        stage_up = gating[:, :, :].rearrange("p a b -> p (a b)")
        stage_gate = hidden_hi[:, :, :].rearrange("p a b -> p (a b)").bitcast(F32)
        stage_down = hidden_lo[:, :, :].rearrange("p a b -> p (a b)").bitcast(F32)

        ring = [ctx.enter_context(nc.psum_tensor(f"ring{i}", [P, 512], F32)) for i in range(RING)]
        max_bank = [ctx.enter_context(nc.psum_tensor(f"max_bank{i}", [P, 512], F32)) for i in range(2)]
        acc = [ctx.enter_context(nc.psum_tensor(f"acc{i}", [P, 512], F32)) for i in range(2)]

        ring_filled = [sem(f"ring_filled{i}") for i in range(RING)]
        ring_drained = [sem(f"ring_drained{i}") for i in range(RING)]
        max_filled = [sem(f"max_filled{i}") for i in range(2)]
        max_drained = [sem(f"max_drained{i}") for i in range(2)]
        acc_filled = [sem(f"acc_filled{i}") for i in range(2)]
        acc_drained = [sem(f"acc_drained{i}") for i in range(2)]
        weights_in = [sem(f"weights_in{i}") for i in range(4)]
        dve_passed, pool_passed, sp_passed = sem("dve_passed"), sem("pool_passed"), sem("sp_passed")
        consts_set = sem("consts_set")
        dve_consts = sem("dve_consts")
        pool_step = sem("pool_step")
        q_bias_scaled = sem("q_bias_scaled")
        abs_summed = sem("abs_summed")
        quant_step = sem("quant_step")
        ternary_done = sem("ternary_done")
        ternary_down_step = sem("ternary_down_step")
        x_in = sem("x_in")
        res_in = sem("res_in")
        res_biased = sem("res_biased")
        qk_hi_done = sem("qk_hi_done")
        qk_rest_done = [sem(f"qk_rest_done{i}") for i in range(FT)]
        qk_mid_done = [sem(f"qk_mid_done{i}") for i in range(FT)]
        qk_split = [sem(f"qk_split{i}") for i in range(FT)]
        parts_written = [sem(f"parts_written{t}") for t in range(QK_TILES)]
        stack_in = [sem(f"stack_in{i}") for i in range(FT)]
        max_hi_done = sem("max_hi_done")
        max_in = [sem(f"max_in{g}") for g in range(QUADS)]
        masked = sem("masked")
        inverted = sem("inverted")
        stats_done = sem("stats_done")
        moments_done = sem("moments_done")
        var_done = sem("var_done")
        rstd_done = sem("rstd_done")
        x1_done = sem("x1_done")
        x1_hi_done = sem("x1_hi_done")
        tanh_done = sem("tanh_done")
        hidden_hi_done = sem("hidden_hi_done")
        hidden_split = sem("hidden_split")
        y_done = sem("y_done")
        y_stored = sem("y_stored")

        STACK_DMAS = 16 * 2 * len(STACK_RUNS)
        MAX_DMAS = 16 * 2

        def at_least(eng, semaphore, per_batch, batch, k):
            if isinstance(batch, int) and per_batch * batch + k == 0:
                return
            eng.wait_ge(semaphore, batch * per_batch + k)

        class Ring:

            def __init__(self, steps, it):
                self.it = it
                self.at = {s: n for n, s in enumerate(s for s in steps if takes_bank(s))}

            def slot(self, step):
                if isinstance(self.it, int) and self.it == 0:
                    return self.at[step] % RING
                return (RING_FIRST + self.at[step]) % RING

            def bank(self, step):
                return ring[self.slot(step)]

            def fills(self, step):
                if isinstance(self.it, int) and self.it == 0:
                    return self.at[step] // RING
                return self.it * (RING_LOOP // RING) + (
                    (RING_FIRST + self.at[step]) // RING - RING_LOOP // RING)

            def wait_free(self, eng, step):
                n = self.fills(step)
                if not (isinstance(n, int) and n == 0):
                    eng.wait_ge(ring_drained[self.slot(step)], n)

            def wait_filled(self, eng, step):
                eng.wait_ge(ring_filled[self.slot(step)], self.fills(step) + 1)

            def wait_drained(self, eng, step):
                eng.wait_ge(ring_drained[self.slot(step)], self.fills(step) + 1)

            def filled(self, instruction, step):
                instruction.then_inc(ring_filled[self.slot(step)], 1)

            def drained(self, instruction, step):
                instruction.then_inc(ring_drained[self.slot(step)], 1)

        def max_at(g, n):
            u = g * MAX_UNITS + n
            return u % 2, u // 2

        def part_slot(t, part):
            return 2 - part if t % 2 else part

        MAX_PER_BANK = QUADS * MAX_UNITS // 2

        def iterations(eng, body):
            body(FIRST, 0)
            with eng.Fori(1, BATCH) as it:
                body(LOOP, it)
            body(LAST, BATCH)

        block = ctx.enter_context(nc.Block())

        @block.sync
        def _(sp):
            sp.sem_inc(var_done, 2)
            sp.sem_inc(y_stored, 16)
            sp.dma_start(xin[:, :, :], x[0].rearrange("(t p) d -> p t d", p=P)).then_inc(x_in, 16)
            sp.dma_start(wqkv[:, :, :], w_qkv.rearrange("(t p) n -> p t n", p=P)).then_inc(weights_in[0], 16)
            sp.dma_start(bias_cols[:, :], b_qkv_cols).then_inc(weights_in[0], 16)
            sp.dma_start(bias_v[:, :], b_qkv[2 * HID:3 * HID].unsqueeze(0).broadcast_to([P, HID])).then_inc(weights_in[0], 16)
            sp.dma_start(bias_o[:, :], b_o.unsqueeze(0).broadcast_to([P, HID])).then_inc(weights_in[1], 16)
            sp.dma_start(wo[:, :, :], w_o.rearrange("(t p) n -> p t n", p=P)).then_inc(weights_in[1], 16)
            sp.dma_start(k_stack[DATA_ROWS:P, :, :].bitcast(U16), k_const).then_inc(weights_in[2], 16)
            sp.dma_start(q_stack[DATA_ROWS:P, :, :].bitcast(U16),
                         q_const.unsqueeze(1).broadcast_to([CONST_ROWS, HEADS, SEQ])).then_inc(weights_in[2], 16)

            def sp_at_least(semaphore, per_batch, batch, k):
                at_least(sp, semaphore, per_batch, batch, k)
                sp.sem_inc(sp_passed, 1)

            def body(steps, it):
                rg = Ring(steps, it)
                prev = it - 1
                first = isinstance(it, int) and it == 0
                for step in steps:
                    kind = step[0]
                    if kind == "load_next":
                        sp_at_least(parts_written[0], 16, it, 16)
                        sp.dma_start(xin[:, :, :], x[it + 1].rearrange("(t p) d -> p t d", p=P)).then_inc(x_in, 16)
                    elif kind == "load_res":
                        sp_at_least(var_done, 2, it, 0)
                        sp.dma_start(res[:, :, :], x[prev].rearrange("(t p) d -> p t d", p=P)).then_inc(res_in, 16)
                    elif kind == "stack_write":
                        t = step[1]
                        sp_at_least(qk_split[t // 2], 2, it, t % 2 + 1)
                        sp_at_least(stack_in[t // 2], STACK_DMAS, it, 0)
                        sp.dma_start(scratch[t].rearrange("s p n -> p s n"), qk_parts[:, t, :, :]).then_inc(parts_written[t], 16)
                    elif kind == "stack_read":
                        half = step[1]
                        for t, stack in ((2 * half, q_stack), (2 * half + 1, k_stack)):
                            sp_at_least(parts_written[t], 16, it, 16)
                            if not first:
                                sp_at_least(masked, 2 * QUADS, prev, QUADS * (half + 1))
                            row = 0
                            for slot, n in STACK_RUNS:
                                if t % 2 == 1:
                                    slot = 3 - slot - n
                                sp.dma_start(
                                    stack[row:row + DH * n, HEADS // 2 * half:HEADS // 2 * (half + 1), :],
                                    scratch[t, slot:slot + n].rearrange("s (d h) n -> (s d) h n", d=DH),
                                ).then_inc(stack_in[half], 16)
                                row += DH * n
                        if first and half == 0:
                            sp.dma_start(stage_up, w_up_t.rearrange("(t p) n -> p t n", p=P)).then_inc(weights_in[3], 16)
                            sp.dma_start(stage_gate, w_gate_t.rearrange("(t p) n -> p t n", p=P)).then_inc(weights_in[3], 16)
                            sp.dma_start(stage_down, w_down_t.rearrange("(t p) n -> p t n", p=P)).then_inc(weights_in[3], 16)
                    elif kind == "mt_out":
                        g = step[1]
                        rg.wait_drained(sp, ("mt", g))
                        sp.sem_inc(sp_passed, 1)
                        for part in range(2):
                            sp.dma_start(
                                q_stack[MAX_ROW + part:MAX_ROW + part + 1, 4 * g:4 * g + 4, :],
                                max_parts[0:4 * TT, g, part, :],
                            ).then_inc(max_in[g], 16)
                    elif kind == "store":
                        sp_at_least(y_done, TT, prev, TT)
                        sp.dma_start(out[prev].rearrange("(t p) d -> p t d", p=P), y[:, :, :]).then_inc(y_stored, 16)

            iterations(sp, body)
            sp.wait_ge(x_in, 16 * (BATCH + 1))
            sp.wait_ge(y_stored, 16 * (BATCH + 1))
            for t in range(QK_TILES):
                sp.wait_ge(parts_written[t], 16 * BATCH)

        @block.tensor
        def _(pe):
            def body(steps, it):
                rg = Ring(steps, it)
                prev = it - 1
                first = isinstance(it, int) and it == 0
                for step in steps:
                    kind = step[0]
                    if takes_bank(step):
                        rg.wait_free(pe, step)
                        bank = rg.bank(step)
                    if kind == "tx":
                        f = step[1]
                        if f == 0:
                            at_least(pe, x_in, 16, it, 16)
                            if first:
                                pe.wait_ge(consts_set, 1)
                        for t in range(TT):
                            mm = pe.transpose(bank[:, P * t:P * (t + 1)], xin[:, t, P * f:P * (f + 1)], ident[:, :])
                        rg.filled(mm, step)
                    elif kind == "qk":
                        t = step[1]
                        if t == 0:
                            rg.wait_drained(pe, ("tx", 0))
                            rg.wait_drained(pe, ("tx", 1))
                            if first:
                                pe.wait_ge(weights_in[0], 48)
                        col = HID * (t % 2) + P * (t // 2)
                        for f in range(FT):
                            mm = pe.matmul(bank[:, :], wqkv[:, f, col:col + P], x_t[:, f, :], start=(f == 0), stop=(f == FT - 1))
                        rg.filled(mm, step)
                    elif kind == "v":
                        t = step[1]
                        for f in range(FT):
                            mm = pe.matmul(bank[:, 0:HID], x_t[:, f, P * t:P * (t + 1)], wqkv[:, f, 2 * HID:3 * HID],
                                           start=(f == 0), stop=(f == FT - 1))
                        rg.filled(mm, step)
                    elif kind == "max":
                        _, g, n = step
                        k, use = max_at(g, n)
                        if n == 0 and g % 2 == 0:
                            at_least(pe, stack_in[g // 2], STACK_DMAS, it, STACK_DMAS)
                            if first:
                                pe.wait_ge(weights_in[2], 32)
                        at_least(pe, max_drained[k], MAX_PER_BANK, it, use)
                        heads, tile = max_unit(n)
                        width = P * (tile + 1)
                        for i, h in enumerate(heads):
                            o = max_bank[k][:, width * i:width * (i + 1)]
                            pe.matmul(o, q_stack[0:MAX_ROW, 4 * g + h, P * tile:P * (tile + 1)],
                                      k_stack[0:MAX_ROW, 4 * g + h, 0:width], start=True, stop=False)
                            mm = pe.matmul(o[:, width - P:width], ident_bf[:, :], causal[:, :], start=False, stop=True)
                        mm.then_inc(max_filled[k], 1)
                    elif kind == "mt":
                        g = step[1]
                        if first and g == 0:
                            pe.wait_ge(dve_consts, 1)
                        for n in (MAX_UNITS - 2, MAX_UNITS - 1):
                            k, use = max_at(g, n)
                            at_least(pe, max_drained[k], MAX_PER_BANK, it, use + 1)
                        rg.filled(pe.transpose(bank[:, 0:P], neg_max[:, g, :], ident[:, :]), step)
                    elif kind == "exp":
                        _, g, n = step
                        if n == 0:
                            at_least(pe, max_in[g], MAX_DMAS, prev if of_batch_before(step) else it, MAX_DMAS)
                        for h, j, col in exp_unit(n):
                            mm = pe.matmul(bank[:, col:col + SEQ - P * j], k_stack[:, 4 * g + h, P * j:P * (j + 1)],
                                           q_stack[:, 4 * g + h, P * j:SEQ], start=True, stop=True)
                        rg.filled(mm, step)
                    elif kind == "pv":
                        _, g, j = step
                        batch = prev if of_batch_before(step) else it
                        if j == 0:
                            at_least(pe, masked, 2 * QUADS, batch, 2 * (g + 1))
                            at_least(pe, acc_drained[g % 2], 3, batch, g // 2)
                            if g == 0:
                                rg.wait_drained(pe, ("v", TT - 1))
                        for h in range(4):
                            n, col = piece(h, j)
                            mm = pe.matmul(acc[g % 2][32 * h:32 * (h + 1), P * j:SEQ], v_ones[:, j, 4 * g + h, :],
                                           probs[:, g % 2, n, col:col + SEQ - P * j], start=(j == 0), stop=(j == TT - 1))
                        if j == TT - 1:
                            mm.then_inc(acc_filled[g % 2], 1)
                    elif kind == "nt":
                        g = step[1]
                        batch = prev if of_batch_before(step) else it
                        at_least(pe, acc_drained[g % 2], 3, batch, g // 2 + 1)
                        for t in range(TT):
                            mm = pe.transpose(bank[:, P * t:P * (t + 1)], pv_t[:, g % 2, P * t:P * (t + 1)], ident[:, :])
                        rg.filled(mm, step)
                    elif kind == "at":
                        f = step[1]
                        rg.wait_drained(pe, ("nt", 2 + f))
                        for t in range(TT):
                            mm = pe.transpose(bank[:, P * t:P * (t + 1)], attn[:, t, P * f:P * (f + 1)], ident[:, :])
                        rg.filled(mm, step)
                    elif kind == "wo":
                        _, u, f = step
                        bank = rg.bank(("wo", u, 0))
                        if u == 0:
                            rg.wait_drained(pe, ("at", f))
                            pe.wait_ge(weights_in[1], 32)
                        for i in range(2):
                            mm = pe.matmul(bank[:, HID * i:HID * (i + 1)], attn_t[:, f, P * (2 * u + i):P * (2 * u + i + 1)],
                                           wo[:, f, :], start=(f == 0 and i == 0), stop=(f == FT - 1), skip_group_check=True)
                        if f == FT - 1:
                            rg.filled(mm, ("wo", u, 0))
                    elif kind == "x1t":
                        u = step[1]
                        at_least(pe, x1_done, TT, prev, 2 * u + 2)
                        for f in range(FT):
                            for i in range(2):
                                mm = pe.transpose(bank[:, HID * f + P * i:HID * f + P * (i + 1)],
                                                  x1[:, 2 * u + i, P * f:P * (f + 1)], ident[:, :])
                        rg.filled(mm, step)
                    elif kind in ("up", "gate"):
                        m = step[1]
                        w = tern_up if kind == "up" else tern_gate
                        if step == ("up", 0):
                            at_least(pe, x1_hi_done, TT // 2, prev, TT // 2)
                            pe.wait_ge(ternary_done, 2)
                        for part in (x1_hi, x1_lo):
                            if step == ("up", 0) and part is x1_lo:
                                rg.wait_drained(pe, ("x1t", 1))
                            for f in range(FT):
                                mm = pe.matmul(bank[:, :], w[:, f, P * m:P * (m + 1)], part[:, f, :],
                                               start=(f == 0 and part is x1_hi), stop=(f == FT - 1 and part is x1_lo))
                        rg.filled(mm, step)
                    elif kind == "down":
                        m = step[1]
                        if m == 0:
                            pe.wait_ge(ternary_down_step, 3)
                            for k in range(2):
                                at_least(pe, acc_drained[k], 3, prev, 2)
                        at_least(pe, hidden_split, ET, prev, m + 1)
                        for t in range(TT):
                            for part in (hidden_hi, hidden_lo):
                                mm = pe.matmul(acc[t // 2][:, HID * (t % 2):HID * (t % 2 + 1)], part[:, m, P * t:P * (t + 1)],
                                               tern_down[:, m, :], start=(m == 0 and part is hidden_hi and t % 2 == 0),
                                               stop=(m == ET - 1 and part is hidden_lo), skip_group_check=True)
                            if m == ET - 1 and t % 2 == 1:
                                mm.then_inc(acc_filled[t // 2], 1)
                    elif kind == "wsum":
                        pe.wait_ge(abs_summed, 3)
                        pe.wait_ge(dve_consts, 1)
                        rg.filled(pe.matmul(bank[:, 0:3], ones[:, :], abs_sums[:, :], start=True, stop=True), step)

            iterations(pe, body)

        @block.scalar
        def _(act):
            def body(steps, it):
                rg = Ring(steps, it)
                prev = it - 1
                first = isinstance(it, int) and it == 0
                for step in steps:
                    kind = step[0]
                    if step == ("tx", 0):
                        rg.wait_filled(act, step)
                        rg.drained(act.activation(x_t[:, 0, :], rg.bank(step)[:, :], ACT.Copy), step)
                    elif kind == "qk" and step[1] >= 2:
                        t = step[1]
                        if first and t == 2:
                            act.wait_ge(q_bias_scaled, 1)
                        scale = DH ** -0.5 if t % 2 == 0 else 1.0
                        bias = bias_cols[:, FT * (t % 2) + t // 2:FT * (t % 2) + t // 2 + 1]
                        at_least(act, parts_written[t], 16, it, 0)
                        rg.wait_filled(act, step)
                        act.activation(qk_parts[:, t, part_slot(t, 0), :], rg.bank(step)[:, :], ACT.Identity, bias=bias, scale=scale)
                        rg.drained(act.activation(qk_rest[:, t, :], rg.bank(step)[:, :], ACT.Identity, bias=bias,
                                                  scale=scale), step)
                    elif kind == "exp":
                        _, g, n = step
                        if n == 0 and not (first and g < 2):
                            at_least(act, acc_filled[g % 2], 3, it if g == 2 else prev, 1 if g >= 2 else 2)
                        rg.wait_filled(act, step)
                        rg.drained(act.activation(probs[:, g % 2, n, :], rg.bank(step)[:, :], ACT.Exp), step)
                    elif kind == "pv" and step[1] < 2 and step[2] == TT - 1:
                        g = step[1]
                        batch = it
                        at_least(act, acc_filled[g % 2], 3, batch, g // 2 + 1)
                        act.activation(pv_t[:, g % 2, :], acc[g % 2][:, :], ACT.Copy).then_inc(acc_drained[g % 2], 1)
                    elif kind == "at":
                        rg.wait_filled(act, step)
                        rg.drained(act.activation(attn_t[:, step[1], :], rg.bank(step)[:, :], ACT.Copy), step)
                    elif kind == "x1t":
                        u = step[1]
                        rg.wait_filled(act, step)
                        act.activation(x1_hi[:, :, 2 * P * u:2 * P * (u + 1)],
                                       rg.bank(step)[:, :].rearrange("p (f n) -> p f n", f=FT), ACT.Copy).then_inc(x1_hi_done, 1)
                    elif kind == "up":
                        m = step[1]
                        if m >= 2:
                            rg.wait_drained(act, ("up", m - 2))
                        rg.wait_filled(act, step)
                        act.activation(gating[:, m % 2, :], rg.bank(step)[:, :], ACT.Tanh,
                                       scale=tanh_scale[:, 0:1]).then_inc(tanh_done, 1)
                    elif kind == "abs_sum":
                        i = step[1]
                        act.wait_ge(weights_in[3], 48)
                        act.activation((tern_up, tern_gate, tern_down)[i][:, :, :].rearrange("p a b -> p (a b)"),
                                       (stage_up, stage_gate, stage_down)[i], ACT.Abs,
                                       accum_out=abs_sums[:, i:i + 1]).then_inc(abs_summed, 1)
                    elif kind == "hidden_hi":
                        m = step[1]
                        rg.wait_drained(act, ("gate", m))
                        act.activation(hidden_hi[:, m, :], hidden[:, m % 2, :], ACT.Copy).then_inc(hidden_hi_done, 1)

            iterations(act, body)

        @block.vector
        def _(dve):
            dve.memset(ones[:, :], 1.0)
            dve.memset(half_neg[:, :], -0.5)
            dve.memset(neg_max[:, :, :], 0.0)
            dve.memset(v_ones[:, :, :, :], 1.0).then_inc(dve_consts, 1)
            dve.wait_ge(dve_consts, 1)
            dve.wait_ge(weights_in[0], 48)
            dve.tensor_scalar(bias_cols[:, 0:FT], bias_cols[:, 0:FT], DH ** -0.5, None, ALU.mult).then_inc(q_bias_scaled, 1)
            dve.wait_ge(q_bias_scaled, 1)

            def normalise(batch, which, target, done):
                at_least(dve, rstd_done, 2, batch, which + 1)
                for t in range(TT):
                    dve.tensor_scalar(target[:, t, :], z[:, t, :], mean_var[:, t, 0:1], rstd[:, t:t + 1],
                                      ALU.subtract, ALU.mult).then_inc(done, 1)

            def moments(batch, which, u):
                tiles = (2 * u, 2 * u + 1)
                for t in tiles:
                    dve.bn_stats(stats[:, t, :], z[:, t, :]).then_inc(stats_done, 1)
                for t in tiles:
                    at_least(dve, stats_done, 2 * TT, batch, which * TT + t + 1)
                    dve.sem_inc(dve_passed, 1)
                    dve.bn_aggr(mean_var[:, t, :], stats[:, t, :]).then_inc(moments_done, 1)
                if u == 1:
                    at_least(dve, moments_done, 2 * TT, batch, (which + 1) * TT)
                    dve.tensor_scalar(var_eps[:, :], mean_var[:, :, 1], LN_EPS, None, ALU.add).then_inc(var_done, 1)

            def body(steps, it):
                rg = Ring(steps, it)
                prev = it - 1
                first = isinstance(it, int) and it == 0
                for step in steps:
                    kind = step[0]
                    if step == ("tx", 1):
                        rg.wait_filled(dve, step)
                        rg.drained(dve.tensor_copy(x_t[:, 1, :], rg.bank(step)[:, :]), step)
                    elif kind == "qk_out":
                        t = step[1]
                        at_least(dve, parts_written[t], 16, it, 0)
                        rg.wait_filled(dve, ("qk", t))
                        rg.drained(dve.tensor_scalar(
                            qk_rest[:, t, :], rg.bank(("qk", t))[:, :], DH ** -0.5 if t == 0 else 1.0,
                            bias_cols[:, FT * (t % 2):FT * (t % 2) + 1], ALU.mult, ALU.add), ("qk", t))
                    elif kind == "split" and step[1] < 2:
                        t = step[1]
                        hi, mid, lo = [qk_parts[:, t, part_slot(t, part), :] for part in range(3)]
                        rg.wait_drained(dve, ("qk", t))
                        dve.tensor_copy(hi, qk_rest[:, t, :]).then_inc(qk_hi_done, 1)
                        at_least(dve, qk_hi_done, 2, it, t + 1)
                        dve.tensor_tensor(qk_rest[:, t, :], qk_rest[:, t, :], hi, ALU.subtract).then_inc(qk_rest_done[0], 1)
                        at_least(dve, qk_rest_done[0], 2, it, t + 1)
                        dve.tensor_copy(mid, qk_rest[:, t, :]).then_inc(qk_mid_done[0], 1)
                        at_least(dve, qk_mid_done[0], 2, it, t + 1)
                        dve.tensor_tensor(lo, qk_rest[:, t, :], mid, ALU.subtract).then_inc(qk_split[0], 1)
                    elif kind == "pv" and step[1] >= 2 and step[2] == TT - 1:
                        g = step[1]
                        at_least(dve, acc_filled[g % 2], 3, prev, g // 2 + 1)
                        dve.tensor_copy(pv_t[:, g % 2, :], acc[g % 2][:, :]).then_inc(acc_drained[g % 2], 1)
                    elif kind == "v_out":
                        v = ("v", step[1])
                        rg.wait_filled(dve, v)
                        rg.drained(dve.tensor_tensor(
                            v_ones[:, step[1], :, 0:DH], rg.bank(v)[:, 0:HID].rearrange("p (h d) -> p h d", d=DH),
                            bias_v[:, :].rearrange("p (h d) -> p h d", d=DH), ALU.add), v)
                    elif kind == "take":
                        _, g, n = step
                        k, use = max_at(g, n)
                        heads, tile = max_unit(n)
                        width = P * (tile + 1)
                        at_least(dve, max_filled[k], MAX_PER_BANK, it, use + 1)
                        first_col = 4 * heads[0] + tile
                        dve.tensor_reduce(
                            neg_max[:, g, first_col:first_col + 4 * (len(heads) - 1) + 1:4],
                            max_bank[k][:, 0:width * len(heads)].rearrange("p (h j) -> p h j", j=width),
                            AX_X, ALU.max, negate=True).then_inc(max_drained[k], 1)
                    elif kind == "mt_out":
                        g = step[1]
                        mt = ("mt", g)
                        at_least(dve, max_in[g], MAX_DMAS, it, 0)
                        rg.wait_filled(dve, mt)
                        m_t = rg.bank(mt)[0:4 * TT, 0:P]
                        dve.tensor_copy(max_parts[0:4 * TT, g, 0, :], m_t).then_inc(max_hi_done, 1)
                        at_least(dve, max_hi_done, QUADS, it, g + 1)
                        rg.drained(dve.tensor_tensor(max_parts[0:4 * TT, g, 1, :], m_t, max_parts[0:4 * TT, g, 0, :],
                                                     ALU.subtract), mt)
                    elif kind == "nt_out":
                        g = step[1]
                        batch = prev if of_batch_before(step) else it
                        nt = ("nt", g)
                        rg.wait_filled(dve, nt)
                        heads = rg.bank(nt)[:, :].rearrange("p (s c) -> p s c", c=32)
                        dve.reciprocal(inv_sum[:, g % 2, :, :], heads[:, :, DH:DH + 1]).then_inc(inverted, 1)
                        at_least(dve, inverted, QUADS, batch, g + 1)
                        rg.drained(dve.tensor_tensor(
                            attn[:, :, 4 * DH * g:4 * DH * (g + 1)].rearrange("p t (h d) -> p t h d", d=DH),
                            heads[:, :, 0:DH].rearrange("p (t h) d -> p t h d", t=TT),
                            inv_sum[:, g % 2, :, :].rearrange("p (t h) o -> p t h o", t=TT).broadcast_to([P, TT, 4, DH]),
                            ALU.mult), nt)
                    elif kind == "wo" and step[2] == FT - 1:
                        u = step[1]
                        bank = ("wo", u, 0)
                        if u == 0:
                            at_least(dve, res_biased, 1, prev, 1)
                        rg.wait_filled(dve, bank)
                        rg.drained(dve.tensor_tensor(
                            z[:, 2 * u:2 * u + 2, :], rg.bank(bank)[:, :].rearrange("p (t d) -> p t d", d=HID),
                            res[:, 2 * u:2 * u + 2, :], ALU.add), bank)
                        rg.wait_drained(dve, bank)
                        moments(prev, 0, u)
                    elif kind == "ln1":
                        normalise(prev, 0, x1, x1_done)
                    elif kind == "x1_lo":
                        u = step[1]
                        x1t = ("x1t", u)
                        tokens = slice(2 * P * u, 2 * P * (u + 1))
                        at_least(dve, x1_hi_done, TT // 2, prev, u + 1)
                        rg.drained(dve.tensor_tensor(x1_lo[:, :, tokens], rg.bank(x1t)[:, :].rearrange("p (f n) -> p f n", f=FT),
                                                     x1_hi[:, :, tokens], ALU.subtract), x1t)
                    elif kind == "swish":
                        m = step[1]
                        up = ("up", m)
                        at_least(dve, tanh_done, ET, prev, m + 1)
                        rg.drained(dve.scalar_tensor_tensor(
                            out=gating[:, 2 + m % 2, :], in0=gating[:, m % 2, :], scalar=1.0, in1=rg.bank(up)[:, :],
                            op0=ALU.add, op1=ALU.mult), up)
                    elif kind == "swiglu":
                        m = step[1]
                        up, gate = ("up", m), ("gate", m)
                        if m >= 2:
                            at_least(dve, hidden_split, ET, prev, m - 1)
                        rg.wait_filled(dve, gate)
                        rg.wait_drained(dve, up)
                        rg.drained(dve.scalar_tensor_tensor(
                            out=hidden[:, m % 2, :], in0=gating[:, 2 + m % 2, :], scalar=HIDDEN_SCALE,
                            in1=rg.bank(gate)[:, :], op0=ALU.mult, op1=ALU.mult), gate)
                    elif kind == "ffn_sum":
                        u = step[1]
                        at_least(dve, acc_filled[u], 3, prev, 3)
                        dve.scalar_tensor_tensor(
                            out=z[:, 2 * u:2 * u + 2, :].rearrange("p t d -> p (t d)"), in0=acc[u][:, :], scalar=ffn_scale[:, 0:1],
                            in1=x1[:, 2 * u:2 * u + 2, :].rearrange("p t d -> p (t d)"), op0=ALU.mult, op1=ALU.add,
                        ).then_inc(acc_drained[u], 1)
                    elif kind == "ffn_stats":
                        u = step[1]
                        at_least(dve, acc_drained[u], 3, prev, 3)
                        moments(prev, 1, u)
                    elif kind == "ln2":
                        at_least(dve, y_stored, 16, it, 0)
                        normalise(prev, 1, y, y_done)
                    elif kind == "wsum":
                        rg.wait_filled(dve, step)
                        rg.drained(dve.tensor_scalar(scales[:, :], rg.bank(step)[:, 0:3], 1.0 / (EXPERT * HID), QUANT_EPS,
                                                     ALU.mult, ALU.add), step)
                        rg.wait_drained(dve, step)
                        dve.tensor_scalar(thresholds[:, :], scales[:, :], 0.5, None, ALU.mult).then_inc(quant_step, 1)
                        dve.tensor_scalar(neg_thresholds[:, :], scales[:, :], -0.5, None, ALU.mult).then_inc(quant_step, 1)
                        dve.tensor_scalar(tanh_scale[:, :], scales[:, 0:1], 0.5, None, ALU.mult).then_inc(quant_step, 1)
                        dve.tensor_scalar(ffn_scale[:, :], scales[:, 1:2], scales[:, 2:3], 1.0 / HIDDEN_SCALE,
                                          ALU.mult, ALU.mult).then_inc(quant_step, 1)
                        dve.wait_ge(quant_step, 4)
                        dve.tensor_tensor(ffn_scale[:, :], ffn_scale[:, :], tanh_scale[:, :], ALU.mult).then_inc(quant_step, 1)
                    elif kind == "ternary" and step[1] < 2:
                        i = step[1]
                        w = (stage_up, stage_gate)[i]
                        t = (tern_up, tern_gate)[i][:, :, :].rearrange("p a b -> p (a b)")
                        dve.tensor_scalar(t, w, neg_thresholds[:, i:i + 1], None, ALU.is_lt).then_inc(quant_step, 1)
                        dve.wait_ge(quant_step, 6 + i)
                        dve.scalar_tensor_tensor(out=t, in0=w, scalar=thresholds[:, i:i + 1], in1=t,
                                                 op0=ALU.is_gt, op1=ALU.subtract).then_inc(ternary_done, 1)

            iterations(dve, body)

        @block.gpsimd
        def _(pool):
            pool.memset(ident[:, :], 0.0).then_inc(pool_step, 1)
            pool.memset(causal[:, :], 0.0).then_inc(pool_step, 1)
            pool.wait_ge(pool_step, 2)
            pool.affine_select(out=ident[:, :], in_=ident[:, :], compare_op=ALU.not_equal, fill=1.0, base=0,
                               pattern=[[-1, P]], channel_multiplier=1).then_inc(pool_step, 1)
            pool.affine_select(out=causal[:, :], in_=causal[:, :], compare_op=ALU.is_ge, fill=MASKED, base=0,
                               pattern=[[-1, P]], channel_multiplier=1).then_inc(pool_step, 1)
            pool.wait_ge(pool_step, 4)
            pool.tensor_copy(ident_bf[:, :], ident[:, :]).then_inc(consts_set, 1)
            pool.wait_ge(dve_consts, 1)

            def keep_past(v, blocks):
                return pool.affine_select(out=v, in_=v, compare_op=ALU.is_ge, fill=0.0, base=0,
                                          pattern=([[0, blocks]] if blocks > 1 else []) + [[1, P]], channel_multiplier=-1)

            def body(steps, it):
                rg = Ring(steps, it)
                prev = it - 1
                for step in steps:
                    kind = step[0]
                    if kind == "load_res":
                        at_least(pool, res_in, 16, prev, 16)
                        pool.wait_ge(weights_in[1], 32)
                        for t in range(TT):
                            ins = pool.tensor_tensor(res[:, t, :], res[:, t, :], bias_o[:, :], ALU.add)
                        ins.then_inc(res_biased, 1)
                    elif kind == "split" and step[1] >= 2:
                        t = step[1]
                        hi, mid, lo = [qk_parts[:, t, part_slot(t, part), :] for part in range(3)]
                        rg.wait_drained(pool, ("qk", t))
                        pool.tensor_tensor(qk_rest[:, t, :], qk_rest[:, t, :], hi, ALU.subtract).then_inc(qk_rest_done[1], 1)
                        at_least(pool, qk_rest_done[1], 2, it, t - 1)
                        pool.sem_inc(pool_passed, 1)
                        pool.tensor_copy(mid, qk_rest[:, t, :]).then_inc(qk_mid_done[1], 1)
                        at_least(pool, qk_mid_done[1], 2, it, t - 1)
                        pool.tensor_tensor(lo, qk_rest[:, t, :], mid, ALU.subtract).then_inc(qk_split[1], 1)
                    elif kind == "ln1" or step == ("ffn_stats", 1):
                        at_least(pool, var_done, 2, it, 1 if kind == "ln1" else 2)
                        pool.tensor_tensor(rstd[:, :], var_eps[:, :], half_neg[:, :], ALU.pow).then_inc(rstd_done, 1)
                    elif kind == "hidden_hi":
                        m = step[1]
                        at_least(pool, hidden_hi_done, ET, prev, m + 1)
                        pool.tensor_tensor(hidden_lo[:, m, :], hidden[:, m % 2, :], hidden_hi[:, m, :],
                                           ALU.subtract).then_inc(hidden_split, 1)
                    elif kind == "ternary" and step[1] == 2:
                        n = step[2]
                        t = tern_down[:, :, :].rearrange("p a b -> p (a b)")
                        if n == 0:
                            pool.wait_ge(quant_step, 4)
                            ins = pool.tensor_scalar(t, stage_down, neg_thresholds[:, 2:3], None, ALU.is_lt)
                        elif n == 1:
                            ins = pool.tensor_scalar(stage_down, stage_down, thresholds[:, 2:3], None, ALU.is_gt)
                        else:
                            pool.wait_ge(ternary_down_step, 2)
                            ins = pool.tensor_tensor(t, stage_down, t, ALU.subtract)
                        ins.then_inc(ternary_down_step, 1)
                    elif kind == "exp" and step[2] % 5 in (1, 3, 4):
                        _, g, n = step
                        rg.wait_drained(pool, step)
                        pool.sem_inc(pool_passed, 1)
                        if n % 5 == 4:
                            both = probs[:, g % 2, n, :].rearrange("p (h q) -> p h q", h=2)
                            keep_past(both[:, :, 0:P], 2).then_inc(masked, 1)
                        else:
                            keep_past(probs[:, g % 2, n - 1:n + 1, 0:P], 2)
                            keep_past(probs[:, g % 2, n, P:2 * P], 1)

            iterations(pool, body)


def bf16_parts(values):
    parts = []
    for _ in range(3):
        bits = values.view(np.uint32) & np.uint32(0xFFFF0000)
        parts.append((bits >> np.uint32(16)).astype(np.uint16))
        values = values - bits.view(np.float32)
    return parts


def constant_rows():
    one, masked = 0x3F80, bf16_parts(np.asarray([MASKED], np.float32))[0][0]
    slopes = np.asarray([1.0 / 2 ** (k / 2) for k in range(HEADS)], np.float32)
    position = np.arange(SEQ)
    k_rows = np.zeros((CONST_ROWS, HEADS, SEQ), np.uint16)
    q_rows = np.zeros((CONST_ROWS, SEQ), np.uint16)
    k_rows[0:3] = bf16_parts(slopes[:, None] * position.astype(np.float32)[None, :])
    q_rows[0:3] = one
    for group in range(MAX_ROW - DATA_ROWS - 3):
        q_rows[3 + group, position // GROUP == group] = one
        k_rows[3 + group, :, position // GROUP > group] = masked
    k_rows[MAX_ROW - DATA_ROWS:MAX_ROW - DATA_ROWS + 2] = one
    return k_rows, q_rows


def kernel(L0_attn_x, L0_attn_Wqkv, L0_attn_bqkv, L0_attn_Wo, L0_attn_bo, L0_ffn_W_up, L0_ffn_W_gate, L0_ffn_W_down):
    import concourse.bacc as bacc
    from concourse.bass_utils import run_bass_kernel_spmd

    def by_dimension(a):
        a = np.array(a)
        qk = a[..., :2 * HID].reshape(a.shape[:-1] + (QK_TILES, HEADS // 2, DH))
        a[..., :2 * HID] = np.swapaxes(qk, -1, -2).reshape(a.shape[:-1] + (2 * HID,))
        return a

    k_rows, q_rows = constant_rows()
    w_qkv, b_qkv = by_dimension(L0_attn_Wqkv), by_dimension(L0_attn_bqkv)
    arrays = {
        "x_dram": np.concatenate([L0_attn_x, np.zeros((1, SEQ, HID), np.float32)]),
        "w_qkv_dram": w_qkv,
        "b_qkv_dram": b_qkv,
        "b_qkv_cols_dram": np.ascontiguousarray(b_qkv.reshape(3 * FT, P).T),
        "w_o_dram": np.ascontiguousarray(L0_attn_Wo),
        "b_o_dram": np.ascontiguousarray(L0_attn_bo),
        "w_up_dram": np.ascontiguousarray(np.asarray(L0_ffn_W_up).T),
        "w_gate_dram": np.ascontiguousarray(np.asarray(L0_ffn_W_gate).T),
        "w_down_dram": np.ascontiguousarray(np.asarray(L0_ffn_W_down).T),
        "k_const_dram": k_rows,
        "q_const_dram": q_rows,
    }
    nc = bacc.Bacc("TRN2", target_bir_lowering=False, num_devices=1)
    args = [nc.dram_tensor(name, a.shape, mybir.dt.from_np(a.dtype), kind="ExternalInput").ap() for name, a in arrays.items()]
    out = nc.dram_tensor("out_dram", (BATCH, SEQ, HID), F32, kind="ExternalOutput").ap()
    scratch = nc.dram_tensor("qk_scratch", (QK_TILES, 3, P, SEQ), BF16, kind="Internal").ap()
    block_kernel(nc, *args, out, scratch)
    r = run_bass_kernel_spmd(nc, [arrays], core_ids=[0])
    return r.results[0]["out_dram"]
```
